# Optimizing a Trainium2 kernel written in Bass

```python
import numpy as np
import jax
import jax.numpy as jnp

def _softmax(x, axis=-1):
    return jax.nn.softmax(x, axis=axis)

def _gelu(x):
    return jax.nn.gelu(x, approximate=True)

def _silu(x):
    return jax.nn.silu(x)

def _sigmoid(x):
    return jax.nn.sigmoid(x)

def _layernorm(x, axis=-1, eps=1e-05):
    m = jnp.mean(x, axis=axis, keepdims=True)
    v = jnp.var(x, axis=axis, keepdims=True)
    return (x - m) / jnp.sqrt(v + eps)

def _scatter_add(tgt, idx, src, axis=0):
    return tgt.at[idx].add(src)

def _segment_sum(src, seg, n):
    return jax.ops.segment_sum(src, seg, n)
kernel_name = 'mk_hybrid_d1_jaxref_r4_33d7ad'

def setup_inputs(seed: int=0):
    np.random.seed(seed)
    _w = jnp.asarray

    def _L0_attn_a_setup():
        import jax, jax.numpy as jnp
        import numpy as np
        H = 16

        def _pairwise_l2(pos):
            sq = jnp.sum((pos[:, :, None, :] - pos[:, None, :, :]) ** 2, axis=-1)
            safe = jnp.where(sq > 0, sq, 1.0)
            return jnp.where(sq > 0, jnp.sqrt(safe), 0.0)
        key = jax.random.key(seed)
        ks = jax.random.split(key, 12)
        B, S, D = (2, 512, 256)
        init = lambda k, shape: jax.random.normal(k, shape, dtype=jnp.float32) * 0.02
        return {'x': jax.random.normal(ks[0], (B, S, D), dtype=jnp.float32), 'wq': init(ks[1], (D, D)), 'bq': init(ks[2], (D,)), 'wk': init(ks[3], (D, D)), 'bk': init(ks[4], (D,)), 'wv': init(ks[5], (D, D)), 'bv': init(ks[6], (D,)), 'wo': init(ks[7], (D, D)), 'bo': init(ks[8], (D,)), 'w3d': init(ks[9], (3, D)), 'b3d': init(ks[10], (3,))}
    _L0_attn_a_in = _L0_attn_a_setup()

    def _L0_attn_b_setup():
        import jax, jax.numpy as jnp
        import numpy as np
        import math
        EMBED_DIM = 256
        N_HEADS = 16
        HEAD_DIM = EMBED_DIM // N_HEADS
        B, N = (2, 512)
        key = jax.random.key(seed)
        k1, k2, k3 = jax.random.split(key, 3)
        x = jax.random.normal(k1, (B, N, EMBED_DIM), dtype=jnp.float32)
        bound = 1.0 / math.sqrt(EMBED_DIM)
        Wkqv = jax.random.uniform(k2, (N_HEADS, EMBED_DIM, 3 * HEAD_DIM), dtype=jnp.float32, minval=-bound, maxval=bound)
        bkqv = jax.random.uniform(k3, (N_HEADS, 3 * HEAD_DIM), dtype=jnp.float32, minval=-bound, maxval=bound)
        return {'x': x, 'Wkqv': Wkqv, 'bkqv': bkqv}
    _L0_attn_b_in = _L0_attn_b_setup()

    def _L0_ffn_setup():
        import jax, jax.numpy as jnp
        import numpy as np
        DIM = 256

        def _reference_tuple_inner(x, W_r, W_k, W_v, mu_r, mu_k):
            B, T, C = x.shape
            x_prev = jnp.concatenate([jnp.zeros((B, 1, C), x.dtype), x[:, :-1, :]], axis=1)
            xr = mu_r * x + (1.0 - mu_r) * x_prev
            xk = mu_k * x + (1.0 - mu_k) * x_prev
            r = jax.nn.sigmoid(jnp.einsum('btc,dc->btd', xr, W_r))
            k = jnp.einsum('btc,dc->btd', xk, W_k)
            k_act = jnp.square(jax.nn.relu(k))
            out = r * jnp.einsum('btc,dc->btd', k_act, W_v)
            new_state = x[:, -1, :]
            return (out, new_state)
        key = jax.random.key(seed)
        ks = jax.random.split(key, 6)
        B, T, C = (8, 512, DIM)
        x = jax.random.normal(ks[0], (B, T, C), dtype=jnp.float32)
        s = 1.0 / np.sqrt(C)
        W_r = jax.random.uniform(ks[1], (C, C), jnp.float32, -s, s)
        W_k = jax.random.uniform(ks[2], (C, C), jnp.float32, -s, s)
        W_v = jax.random.uniform(ks[3], (C, C), jnp.float32, -s, s)
        mu_r = jax.random.uniform(ks[4], (C,), jnp.float32)
        mu_k = jax.random.uniform(ks[5], (C,), jnp.float32)
        return {'x': x, 'W_r': W_r, 'W_k': W_k, 'W_v': W_v, 'mu_r': mu_r, 'mu_k': mu_k}
    _L0_ffn_in = _L0_ffn_setup()
    _d = {'L0_attn_a_x': _L0_attn_a_in['x'], 'L0_attn_a_wq': _L0_attn_a_in['wq'], 'L0_attn_a_bq': _L0_attn_a_in['bq'], 'L0_attn_a_wk': _L0_attn_a_in['wk'], 'L0_attn_a_bk': _L0_attn_a_in['bk'], 'L0_attn_a_wv': _L0_attn_a_in['wv'], 'L0_attn_a_bv': _L0_attn_a_in['bv'], 'L0_attn_a_wo': _L0_attn_a_in['wo'], 'L0_attn_a_bo': _L0_attn_a_in['bo'], 'L0_attn_a_w3d': _L0_attn_a_in['w3d'], 'L0_attn_a_b3d': _L0_attn_a_in['b3d'], 'L0_attn_b_Wkqv': _L0_attn_b_in['Wkqv'], 'L0_attn_b_bkqv': _L0_attn_b_in['bkqv'], 'L0_ffn_W_r': _L0_ffn_in['W_r'], 'L0_ffn_W_k': _L0_ffn_in['W_k'], 'L0_ffn_W_v': _L0_ffn_in['W_v'], 'L0_ffn_mu_r': _L0_ffn_in['mu_r'], 'L0_ffn_mu_k': _L0_ffn_in['mu_k']}
    _x0 = _d['L0_attn_a_x']
    _d['L0_attn_a_x'] = jax.random.normal(jax.random.fold_in(jax.random.key(seed), 1), (8, 1024, 256), dtype=_x0.dtype)
    del _x0
    return _d

def reference(L0_attn_a_x, L0_attn_a_wq, L0_attn_a_bq, L0_attn_a_wk, L0_attn_a_bk, L0_attn_a_wv, L0_attn_a_bv, L0_attn_a_wo, L0_attn_a_bo, L0_attn_a_w3d, L0_attn_a_b3d, L0_attn_b_Wkqv, L0_attn_b_bkqv, L0_ffn_W_r, L0_ffn_W_k, L0_ffn_W_v, L0_ffn_mu_r, L0_ffn_mu_k):

    def _L0_attn_a_ref(x, wq, bq, wk, bk, wv, bv, wo, bo, w3d, b3d):
        import jax, jax.numpy as jnp
        import numpy as np
        H = 16

        def _pairwise_l2(pos):
            sq = jnp.sum((pos[:, :, None, :] - pos[:, None, :, :]) ** 2, axis=-1)
            safe = jnp.where(sq > 0, sq, 1.0)
            return jnp.where(sq > 0, jnp.sqrt(safe), 0.0)
        B, S, D = x.shape
        hd = D // H
        scale = 1.0 / hd ** 0.5
        V = (x @ wv.T + bv).reshape(B, S, H, hd).transpose(0, 2, 1, 3)
        pos = x @ w3d.T + b3d
        dist = _pairwise_l2(pos)
        scores = -dist[:, None, :, :] * scale
        causal = jnp.triu(jnp.ones((S, S), dtype=bool), k=1)
        scores = jnp.where(causal[None, None], -jnp.inf, scores)
        attn = jax.nn.softmax(scores, axis=-1)
        attn = jnp.nan_to_num(attn, nan=0.0)
        out = jnp.einsum('bhqk,bhkd->bhqd', attn, V)
        out = out.transpose(0, 2, 1, 3).reshape(B, S, D)
        return out @ wo.T + bo

    def _L0_attn_b_ref(x, Wkqv, bkqv):
        import jax, jax.numpy as jnp
        import numpy as np
        import math
        EMBED_DIM = 256
        N_HEADS = 16
        HEAD_DIM = EMBED_DIM // N_HEADS
        B, N = (2, 512)
        Bx, Nx, D = x.shape
        hd = Wkqv.shape[-1] // 3
        proj = jnp.einsum('bnd,hdf->bhnf', x, Wkqv) + bkqv[None, :, None, :]
        k, q, v = jnp.split(proj, 3, axis=-1)
        scores = jnp.einsum('bhqd,bhkd->bhqk', q, k) / math.sqrt(hd)
        causal = jnp.tril(jnp.ones((Nx, Nx), dtype=bool))
        scores = jnp.where(causal[None, None, :, :], scores, -jnp.inf)
        attn = jax.nn.softmax(scores, axis=-1)
        out = jnp.einsum('bhqk,bhkd->bhqd', attn, v)
        return out.transpose(0, 2, 1, 3).reshape(Bx, Nx, D)

    def _L0_ffn_ref(x, W_r, W_k, W_v, mu_r, mu_k):
        import jax, jax.numpy as jnp
        import numpy as np
        DIM = 256

        def _reference_tuple_inner(x, W_r, W_k, W_v, mu_r, mu_k):
            B, T, C = x.shape
            x_prev = jnp.concatenate([jnp.zeros((B, 1, C), x.dtype), x[:, :-1, :]], axis=1)
            xr = mu_r * x + (1.0 - mu_r) * x_prev
            xk = mu_k * x + (1.0 - mu_k) * x_prev
            r = jax.nn.sigmoid(jnp.einsum('btc,dc->btd', xr, W_r))
            k = jnp.einsum('btc,dc->btd', xk, W_k)
            k_act = jnp.square(jax.nn.relu(k))
            out = r * jnp.einsum('btc,dc->btd', k_act, W_v)
            new_state = x[:, -1, :]
            return (out, new_state)
        return _reference_tuple_inner(x, W_r, W_k, W_v, mu_r, mu_k)[0]
    x = L0_attn_a_x
    x = x + _L0_attn_a_ref(_layernorm(x, axis=-1), L0_attn_a_wq, L0_attn_a_bq, L0_attn_a_wk, L0_attn_a_bk, L0_attn_a_wv, L0_attn_a_bv, L0_attn_a_wo, L0_attn_a_bo, L0_attn_a_w3d, L0_attn_a_b3d)
    x = x + _L0_ffn_ref(_layernorm(x, axis=-1), L0_ffn_W_r, L0_ffn_W_k, L0_ffn_W_v, L0_ffn_mu_r, L0_ffn_mu_k)
    x = x + _L0_attn_b_ref(_layernorm(x, axis=-1), L0_attn_b_Wkqv, L0_attn_b_bkqv)
    x = x + _L0_ffn_ref(_layernorm(x, axis=-1), L0_ffn_W_r, L0_ffn_W_k, L0_ffn_W_v, L0_ffn_mu_r, L0_ffn_mu_k)
    return x

_drawn_inputs = setup_inputs


def setup_inputs(seed=0):
    import zlib

    import numpy as np

    out = dict(_drawn_inputs(seed))
    spreads = {}
    factors = {'L0_attn_a_wv': 5.183,
     'L0_attn_a_bv': 7.687,
     'L0_attn_a_wo': 4.174,
     'L0_attn_a_w3d': 8.0,
     'L0_attn_a_b3d': 64.0,
     'L0_ffn_mu_r': 3.232,
     'L0_attn_a_bo': 2.727}
    for name, (base, spread) in spreads.items():
        noise = np.random.default_rng([zlib.crc32(name.encode()), seed]).standard_normal(out[name].shape)
        drawn = base * np.exp(spread * noise) if base else spread * noise
        out[name] = jnp.asarray(drawn.astype(out[name].dtype))
    for name, factor in factors.items():
        out[name] = (out[name] * factor).astype(out[name].dtype)
    return out
```

```python
from contextlib import ExitStack

import concourse.bass as bass
from concourse import mybir

F32 = mybir.dt.float32
BF16 = mybir.dt.bfloat16
ALU = mybir.AluOpType
ACT = mybir.ActivationFunctionType
AX = mybir.AxisListType

P = 128
B, S, C = 8, 1024, 256
H, HD = 16, 16
NT = S // P
NC = C // P
HALF = S // 2
TPH = HALF // P
GH = 4
NG = H // GH
H8 = P // HD
NHT = H // H8
EPS = 1e-5
SCALE = HD ** -0.5
TINY = 1e-30
LOWEST = -3.0e38
VC = C + 4
POS, ONE = C, C + 3
VW = HD + 1

HI, MID, LO = 0, 1, 2
K_SLOTS = (HI, MID, LO, HI, MID, HI)
Q_SLOTS = (HI, HI, HI, MID, MID, LO)
KROWS = HD * len(K_SLOTS)
SROWS = KROWS + 2
STACKS = 3
STACK_OF = (0, 1, 2, 0)
STACK_LOADS = (2, 1, 1)
STACK_NTH = (0, 0, 0, 1)
N_STACK_DMA = 9

KEY_PIECES = [(kt, P * kt, HALF) for kt in range(TPH)] + \
             [(kt, max(HALF, P * kt), S) for kt in range(NT)]
DIAGONAL = [q0 == P * kt for kt, q0, _ in KEY_PIECES]
NTH_DIAGONAL = [sum(DIAGONAL[:m]) for m in range(len(KEY_PIECES))]
QUERY_PIECES = [(i, 0, P * (i + 1)) for i in range(TPH)] + \
               [(i, 0, HALF) for i in range(TPH, NT)] + \
               [(i, HALF, P * (i + 1)) for i in range(TPH, NT)]
NP = len(KEY_PIECES)
assert NP == len(QUERY_PIECES) == 12
LEAD = NP + 3
SLOTS = NG * NP + LEAD + 4
P1_AT = [sum(S - P * j for j in range(kt)) for kt in range(NT)]
P1_COLS = sum(S - P * j for j in range(NT))


def bass_hybrid(nc, x, wq, bq, wk, bk, wv, bv, wo, bo, w3d, b3d, wkqv, bkqv, w_r, w_k, w_v,
                mu_r, mu_k, out):
    parts_dram = nc.dram_tensor("parts_dram", [B, 2, NHT, 3, HD, H8, S], BF16, kind="Internal").ap()

    nc.disable_value_cache = True

    with ExitStack() as ctx:
        def sb(name, shape, dt=F32):
            return ctx.enter_context(nc.sbuf_tensor(name, shape, dt))

        def psum(name):
            return ctx.enter_context(nc.psum_tensor(name, [P, HALF], F32))

        def sem(name):
            return ctx.enter_context(nc.semaphore(name))

        side = [psum(f"side{k}") for k in range(2)]
        max_bank = [psum(f"max_bank{k}") for k in range(2)]
        exp_bank = [psum(f"exp_bank{k}") for k in range(2)]
        o_bank = [psum(f"o_bank{k}") for k in range(2)]

        ident = sb("ident", [P, P])
        identb = sb("identb", [P, P], BF16)
        mask = sb("mask", [P, HALF])
        wvp = sb("wvp", [P, NC, C + 3])
        bias_vp = sb("bias_vp", [P, C + 3])
        wrT = sb("wrT", [P, NC, C])
        wkT = sb("wkT", [P, NC, C])
        wvT = sb("wvT", [P, NC, C])                      
        wkq = sb("wkq", [P, NC, 2, NHT, HD, H8])
        wv3 = sb("wv3", [P, NC, H, HD])
        bv3 = sb("bv3", [P, H, HD])
        cols = sb("cols", [P, 10])
        BV, MUR, MUK, BKQ = 0, 2, 4, 6

        xa = sb("xa", [P, NT, C])
        xb = sb("xb", [P, NT, C])
        xha = sb("xha", [P, TPH, C])
        xhb = sb("xhb", [P, TPH, C])
        xta = sb("xta", [P, NC, S])
        xtb = sb("xtb", [P, NC, 1 + S])
        st = sb("st", [P, TPH, 6])
        mv = sb("mv", [P, TPH, 2])
        var_eps = sb("var_eps", [P, TPH])
        rstd = sb("rstd", [P, TPH])
        minus_half = sb("minus_half", [P, TPH])
        vp = sb("vp", [P, NT, VC])
        neg_pos = sb("neg_pos", [P, NT, 3])
        pb = sb("pb", [P, 3, S])
        sq = sb("sq", [P, 2, 3, HALF])
        p1 = sb("p1", [P, P1_COLS])
        rinv1 = sb("rinv1", [P, NT])
        xr, xk, ka = (pb[:, k, :].rearrange("p (c n) -> p c n", c=NC) for k in range(3))
        kr = sq[:, 0, 0:2, :]
        th = sq[:, 1, 0:2, :].rearrange("p a (b c) -> p (a b) c", c=C)
        tm = sb("tm", [P, TPH, C])
        x32 = sb("x32", [P, 2, HALF])
        parts = sb("parts", [P, 2, 3, HALF], BF16)
        v3 = sb("v3", [P, NT, H, VW])
        ks = [sb(f"ks{r}", [SROWS, GH, S], BF16) for r in range(STACKS)]
        qs = [sb(f"qs{r}", [SROWS, GH, S], BF16) for r in range(STACKS)]
        piece_max = sb("piece_max", [P, GH, NP])
        neg_max = sb("neg_max", [P, 2, GH, NT], BF16)
        neg_maxT = sb("neg_maxT", [GH * NT, 2, P], BF16)
        pt = sb("pt", [P, 2, GH, HALF])
        ot = sb("ot", [P, 2, HALF])
        rsum = sb("rsum", [P, TPH, GH])
        on = sb("on", [P, TPH, GH, HD])

        raw = pt[:, :, :, :].rearrange("p a b n -> p (a b n)")[:, 0:5 * NC * C].rearrange(
            "p (w a n) -> p w a n", w=5, a=NC)
        raw3d = ot[0:3, 0, 0:C]
        raw_kqv = p1[:, 0:NC * H * 48].rearrange("p (a h f) -> p a h f", a=NC, h=H)
        rows = sq[0:1, :, :, :].rearrange("p a b n -> p (a b n)")
        bv_row, mur_row, muk_row = (rows[:, k * C:(k + 1) * C] for k in range(3))
        kqv_row = rows[:, 3 * C:3 * C + H * 48].rearrange("p (t h f) -> p t h f", t=NHT, h=H8)
        bkq_row = rows[:, 3 * C + H * 48:3 * C + H * 48 + 2 * C].rearrange(
            "p (q t d h) -> p q t d h", q=2, t=NHT, d=HD)
        bo_all = tm[:, 0, :]
        bv_wide = tm[:, 1, :].rearrange("p (a n) -> p a n", a=NC)

        raw_loaded, rows_loaded, cleared, consts_ready, rows_ready, bv_spread, weights_ready = (
            sem(n) for n in ("raw_loaded", "rows_loaded", "cleared", "consts_ready", "rows_ready",
                             "bv_spread", "weights_ready"))
        setup_full, setup_taken = sem("setup_full"), sem("setup_taken")
        x_loaded = [sem(f"x_loaded{h}") for h in range(2)]
        xb_copied = sem("xb_copied")
        out_stored = sem("out_stored")
        STAGES = ("att1", "ffn2", "proj3", "ffn4")
        ln_step = {s: sem(f"{s}_ln_step") for s in STAGES}
        rstd_ready = {s: sem(f"{s}_rstd_ready") for s in STAGES}
        xh_ready = {s: sem(f"{s}_xh_ready") for s in STAGES}
        tr_full = {s: sem(f"{s}_tr_full") for s in STAGES}
        xt_ready = {s: sem(f"{s}_xt_ready") for s in STAGES}
        v1_full, vp_ready, neg_ready, pb_full, pb_ready = (
            sem(n) for n in ("v1_full", "vp_ready", "neg_ready", "pb_full", "pb_ready"))
        sq_ready, sum_ready, dist2_ready, log_done, dist_done, p1_exp, p1_sel, pv1_full, rinv_done, x1_done = (
            sem(n) for n in ("sq_ready", "sum_ready", "dist2_ready", "log_done", "dist_done", "p1_exp", "p1_sel",
                             "pv1_full", "rinv_done", "x1_done"))
        FF = ("ffn2", "ffn4")
        diff_done, xr_ready, xk_ready, k_full, r_full, kr_ready, ka_ready, rexp_done, rlog_done, th_ready, v_full, tm_ready, x_added = (
            {s: sem(f"{s}_{n}") for s in FF} for n in (
                "diff_done", "xr_ready", "xk_ready", "k_full", "r_full", "kr_ready", "ka_ready",
                "rexp_done", "rlog_done", "th_ready", "v_full", "tm_ready", "x_added"))
        kq_full, x32_ready, hi_done, rest_done, mid_done, lo_done, v3_full, v3_ready = (
            sem(n) for n in ("kq_full", "x32_ready", "hi_done", "rest_done", "mid_done", "lo_done",
                             "v3_full", "v3_ready"))
        part_stored = [sem(f"part_stored{k}") for k in range(2)]
        stack_ready = [sem(f"stack_ready{r}") for r in range(STACKS)]
        max_full, max_free, c_step, negmax_ready, negmaxT_full, negmaxT_ready, crow_ready = (
            sem(n) for n in ("max_full", "max_free", "c_step", "negmax_ready", "negmaxT_full",
                             "negmaxT_ready", "crow_ready"))
        s_full, exp_done, sel_done, pv_done, ot_ready, on_full, rsum_done, on_ready, xb_added = (
            sem(n) for n in ("s_full", "exp_done", "sel_done", "pv_done", "ot_ready",
                             "on_full", "rsum_done", "on_ready", "xb_added"))
        o_full = [sem(f"o_full{h}") for h in range(2)]
        stats_seen, p1_seen, exp_seen, scores_seen = (
            sem(name) for name in ("stats_seen", "p1_seen", "exp_seen", "scores_seen"))

        x_tok = x.rearrange("b (t p) c -> b p t c", p=P)
        out_tok = out.rearrange("b (t p) c -> b p t c", p=P)


        def dve_normalise(s, src, dst, n, h, ready):
            dve = nc.vector
            base = 6 * n + 3 * h
            ready(h)
            for t in range(TPH):
                last = dve.bn_stats(st[:, t, :], src[:, TPH * h + t, :])
            last.then_inc(ln_step[s], 1)
            dve.wait_ge(ln_step[s], base + 1).then_inc(stats_seen, 1)
            for t in range(TPH):
                last = dve.bn_aggr(mv[:, t, :], st[:, t, :])
            last.then_inc(ln_step[s], 1)
            dve.wait_ge(ln_step[s], base + 2)
            dve.tensor_scalar(var_eps[:, :], mv[:, :, 1], EPS, None, ALU.add).then_inc(ln_step[s], 1)
            dve.wait_ge(rstd_ready[s], 2 * n + h + 1)
            if h == 1:
                dve.wait_ge(tr_full[s], 4 * n + 2)
            for t in range(TPH):
                last = dve.tensor_scalar(dst[:, t, :], src[:, TPH * h + t, :], mv[:, t, 0:1],
                                         rstd[:, t:t + 1], ALU.subtract, ALU.mult)
            last.then_inc(xh_ready[s], 1)

        def dve_att1(n):
            dve = nc.vector

            def loaded(h):
                dve.wait_ge(x_loaded[h], 16 * n + 16)

            def values(t):
                dve.wait_ge(v1_full, 8 * n + t + 1)
                dve.tensor_tensor(vp[:, t, 0:C + 3], side[t % 2][:, 0:C + 3], bias_vp[:, :],
                                  ALU.add).then_inc(vp_ready, 1)

            def negate(h):
                dve.wait_ge(vp_ready, 8 * n + TPH * (h + 1))
                dve.tensor_scalar(neg_pos[:, TPH * h:TPH * (h + 1), :],
                                  vp[:, TPH * h:TPH * (h + 1), POS:POS + 3], -1.0, None,
                                  ALU.mult).then_inc(neg_ready, 1)

            def distance(p):
                kt, q0, q1 = KEY_PIECES[p]
                w = q1 - q0
                dve.wait_ge(sum_ready, NP * n + p + 1)
                dve.scalar_tensor_tensor(out=sq[:, p % 2, 0, 0:w], in0=sq[:, p % 2, 0, 0:w],
                                         scalar=TINY, in1=sq[:, p % 2, 2, 0:w],
                                         op0=ALU.max, op1=ALU.add).then_inc(dist2_ready, 1)

            def residual(t):
                dve.wait_ge(pv1_full, 8 * n + t + 1)
                dve.reciprocal(rinv1[:, t:t + 1], side[t % 2][:, ONE:ONE + 1]).then_inc(rinv_done, 1)
                dve.wait_ge(rinv_done, 8 * n + t + 1)
                dve.scalar_tensor_tensor(out=xa[:, t, :], in0=side[t % 2][:, 0:C],
                                         scalar=rinv1[:, t:t + 1], in1=xa[:, t, :],
                                         op0=ALU.mult, op1=ALU.add).then_inc(x1_done, 1)

            dve_normalise("att1", xa, xha, n, 0, loaded)
            yield
            dve_normalise("att1", xa, xha, n, 1, loaded)
            yield
            values(0)
            values(1)
            yield
            values(2)
            values(3)
            negate(0)
            yield
            values(4)
            values(5)
            yield
            values(6)
            values(7)
            negate(1)
            yield
            yield
            yield
            for p in range(NP + 2):
                if p < NP:
                    distance(p)
                if 2 <= p < 2 + TPH:
                    residual(p - 2)
                if p >= 2 + 2 * TPH:
                    residual(p - 2 - TPH)
                yield

        def dve_ffn(s, src, n, previous):
            dve = nc.vector

            def ready(h):
                if s == "ffn2":
                    dve.wait_ge(x1_done, 8 * n + TPH * (h + 1))
                else:
                    dve.wait_ge(xb_added, 8 * n + 2 * (NG - 1) + h + 1)

            def mix(h):
                dve.wait_ge(diff_done[s], 2 * n + h + 1)
                if h == 1:
                    dve.wait_ge(r_full[s], 4 * n + 2)
                before = xtb[:, :, HALF * h:HALF * h + HALF]
                for dst, mu, done in ((xr, MUR, xr_ready), (xk, MUK, xk_ready)):
                    for c in range(NC):
                        last = dve.scalar_tensor_tensor(
                            out=dst[:, c, :], in0=xk[:, c, :], scalar=cols[:, mu + c:mu + c + 1],
                            in1=before[:, c, :], op0=ALU.mult, op1=ALU.add)
                    last.then_inc(done[s], 1)

            def gate(h):
                if h == 0:
                    dve.wait_ge(*previous)
                else:
                    dve.wait_ge(x_added[s], 2 * n + 1)
                dve.wait_ge(th_ready[s], 2 * n + h + 1)
                for j in range(2):
                    dve.wait_ge(v_full[s], 4 * n + 2 * h + j + 1)
                    dve.tensor_tensor(tm[:, 2 * j:2 * j + 2, :], th[:, 2 * j:2 * j + 2, :],
                                      side[j][:, :].rearrange("p (t c) -> p t c", c=C),
                                      ALU.mult).then_inc(tm_ready[s], 1)

            dve_normalise(s, src, xhb, n, 0, ready)
            yield
            dve_normalise(s, src, xhb, n, 1, ready)
            yield
            mix(0)
            yield
            yield
            yield
            gate(0)
            mix(1)
            yield
            yield
            yield
            gate(1)
            yield

        def dve_proj3(n):
            dve = nc.vector

            def ready(h):
                dve.wait_ge(x_added["ffn2"], 2 * n + h + 1)

            def split(j):
                r = j % 2
                if j >= 2:
                    dve.wait_ge(part_stored[r], 64 * n + 16 * (j // 2))
                else:
                    dve.wait_ge(part_stored[r], 64 * n)
                dve.wait_ge(x32_ready, 8 * n + j + 1)
                dve.tensor_copy(parts[:, r, HI, :], x32[:, r, :]).then_inc(hi_done, 1)
                dve.wait_ge(hi_done, 8 * n + j + 1)
                dve.tensor_tensor(x32[:, r, :], x32[:, r, :], parts[:, r, HI, :],
                                  ALU.subtract).then_inc(rest_done, 1)
                dve.wait_ge(rest_done, 8 * n + j + 1)
                dve.tensor_copy(parts[:, r, MID, :], x32[:, r, :]).then_inc(mid_done, 1)

            dve_normalise("proj3", xa, xha, n, 0, ready)
            yield
            dve_normalise("proj3", xa, xha, n, 1, ready)
            yield
            yield
            for j in range(8):
                split(j)
                yield

        def dve_values3(n):
            for j in range(4):
                nc.vector.wait_ge(v3_full, 4 * n + j + 1)
                for t in range(2):
                    last = nc.vector.tensor_tensor(
                        v3[:, 2 * j + t, :, 0:HD],
                        side[j % 2][:, C * t:C * (t + 1)].rearrange("p (h d) -> p h d", d=HD),
                        bv3[:, :, :], ALU.add)
                last.then_inc(v3_ready, 1)
            yield

        def act_transposed(s, dst, off, n, h):
            for c in range(NC):
                nc.scalar.wait_ge(tr_full[s], 4 * n + 2 * h + c + 1)
                nc.scalar.activation(dst[:, c, off + HALF * h:off + HALF * (h + 1)], side[c][:, :],
                                     ACT.Copy).then_inc(xt_ready[s], 1)

        def act_att1(n):
            act = nc.scalar

            def positions(c, h):
                k = 3 * h + c
                act.wait_ge(pb_full, 6 * n + k + 1)
                act.activation(pb[:, c, HALF * h:HALF * (h + 1)], side[k % 2][:, :],
                               ACT.Copy).then_inc(pb_ready, 1)

            def square(p, c):
                kt, q0, q1 = KEY_PIECES[p]
                w = q1 - q0
                if c == 0:
                    act.wait_ge(neg_ready, 2 * n + kt // TPH + 1)
                    act.wait_ge(pb_ready, 6 * n + (3 if q1 <= HALF else 6))
                    act.wait_ge(p1_exp, NP * n + max(0, p - 1))
                mm = act.activation(sq[:, p % 2, c, 0:w], pb[:, c, q0:q1], ACT.Square,
                                    bias=neg_pos[:, kt, c:c + 1])
                if c == 2:
                    mm.then_inc(sq_ready, 1)

            def step(p):
                if p >= 1:
                    kt, q0, q1 = KEY_PIECES[p - 1]
                    w = q1 - q0
                    d = sq[:, (p - 1) % 2, 0, 0:w]
                    at = P1_AT[kt] + q0 - P * kt
                    act.wait_ge(dist2_ready, NP * n + p)
                    act.activation(d, d, ACT.Ln).then_inc(log_done, 1)
                if p < NP:
                    square(p, 0)
                if p >= 1:
                    act.wait_ge(log_done, NP * n + p)
                    act.activation(d, d, ACT.Exp, scale=0.5).then_inc(dist_done, 1)
                if p < NP:
                    square(p, 1)
                    square(p, 2)
                if p >= 1:
                    if p == 1:
                        act.wait_ge(pv1_full, 8 * n)
                    act.wait_ge(dist_done, NP * n + p)
                    act.activation(p1[:, at:at + w], d, ACT.Exp, scale=-SCALE).then_inc(p1_exp, 1)

            yield
            act.wait_ge(v3_full, 4 * n)
            act_transposed("att1", xta, 0, n, 0)
            yield
            act_transposed("att1", xta, 0, n, 1)
            yield
            yield
            positions(0, 0)
            yield
            positions(1, 0)
            yield
            positions(2, 0)
            positions(0, 1)
            yield
            positions(1, 1)
            positions(2, 1)
            yield
            for p in range(NP + 2):
                if p <= NP:
                    step(p)
                yield

        def act_ffn(s, n):
            act = nc.scalar

            def relu_k(h):
                for j in range(2):
                    act.wait_ge(k_full[s], 4 * n + 2 * h + j + 1)
                    if h == 1:
                        act.wait_ge(ka_ready[s], 4 * n + j + 1)
                    act.activation(kr[:, j, :], side[j][:, :], ACT.Relu).then_inc(kr_ready[s], 1)

            def sigmoid(h):
                if h == 1:
                    act.wait_ge(tm_ready[s], 4 * n + 2)
                for j in range(2):
                    act.wait_ge(r_full[s], 4 * n + 2 * h + j + 1)
                    act.activation(th[:, 2 * j:2 * j + 2, :],
                                   side[j][:, :].rearrange("p (t c) -> p t c", c=C),
                                   ACT.Exp, scale=-1.0).then_inc(rexp_done[s], 1)
                act.wait_ge(rexp_done[s], 4 * n + 2 * h + 2)
                act.activation(th[:, :, :], th[:, :, :], ACT.Ln, bias=1.0).then_inc(rlog_done[s], 1)
                act.wait_ge(rlog_done[s], 2 * n + h + 1)
                act.activation(th[:, :, :], th[:, :, :], ACT.Exp, scale=-1.0).then_inc(th_ready[s], 1)

            yield
            act_transposed(s, xtb, 1, n, 0)
            yield
            act_transposed(s, xtb, 1, n, 1)
            yield
            relu_k(0)
            yield
            sigmoid(0)
            yield
            yield
            relu_k(1)
            yield
            sigmoid(1)
            yield
            yield

        def act_proj3(n):
            act = nc.scalar
            yield
            act_transposed("proj3", xta, 0, n, 0)
            yield
            act_transposed("proj3", xta, 0, n, 1)
            yield
            for j in range(8):
                kq, ht = (j // NHT) % 2, j % NHT
                act.wait_ge(kq_full, 8 * n + j + 1)
                if j >= 2:
                    act.wait_ge(lo_done, 8 * n + j - 1)
                else:
                    act.wait_ge(lo_done, 8 * n)
                act.activation(x32[:, j % 2, :], side[j % 2][:, :], ACT.Identity,
                               bias=cols[:, BKQ + 2 * kq + ht:BKQ + 2 * kq + ht + 1]).then_inc(x32_ready, 1)
                yield

        def pool_rstd(s, n, h):
            nc.gpsimd.wait_ge(ln_step[s], 6 * n + 3 * h + 3)
            nc.gpsimd.tensor_tensor(rstd[:, :], var_eps[:, :], minus_half[:, :],
                                    ALU.pow).then_inc(rstd_ready[s], 1)

        def pool_att1(n):
            pool = nc.gpsimd

            def select(p):
                kt, q0, _ = KEY_PIECES[p]
                if not DIAGONAL[p]:
                    return
                block = p1[:, P1_AT[kt]:P1_AT[kt] + P]
                pool.wait_ge(p1_exp, NP * n + p + 1).then_inc(p1_seen, 1)
                pool.affine_select(out=block, in_=block, compare_op=ALU.is_ge, fill=0.0, base=0,
                                   pattern=[[1, P]], channel_multiplier=-1).then_inc(p1_sel, 1)

            pool_rstd("att1", n, 0)
            yield
            pool_rstd("att1", n, 1)
            for _ in range(7):
                yield
            for p in range(NP + 2):
                if p < NP:
                    w = KEY_PIECES[p][2] - KEY_PIECES[p][1]
                    pool.wait_ge(sq_ready, NP * n + p + 1)
                    pool.tensor_tensor(sq[:, p % 2, 0, 0:w], sq[:, p % 2, 0, 0:w],
                                       sq[:, p % 2, 1, 0:w], ALU.add).then_inc(sum_ready, 1)
                if 1 <= p <= NP:
                    select(p - 1)
                yield

        def pool_ffn(s, src, n):
            pool = nc.gpsimd

            def difference(h):
                pool.wait_ge(xt_ready[s], 4 * n + 2 * h + 2)
                if h == 1:
                    pool.wait_ge(k_full[s], 4 * n + 2)
                lo = HALF * h
                pool.tensor_tensor(xk[:, :, :], xtb[:, :, 1 + lo:1 + lo + HALF], xtb[:, :, lo:lo + HALF],
                                   ALU.subtract).then_inc(diff_done[s], 1)

            def square_k(h):
                for j in range(2):
                    pool.wait_ge(kr_ready[s], 4 * n + 2 * h + j + 1)
                    pool.tensor_tensor(ka[:, j, :], kr[:, j, :], kr[:, j, :],
                                       ALU.mult).then_inc(ka_ready[s], 1)

            def add(h):
                pool.wait_ge(tm_ready[s], 4 * n + 2 * h + 2)
                x_half = src[:, TPH * h:TPH * (h + 1), :]
                pool.tensor_tensor(x_half, x_half, tm[:, :, :], ALU.add).then_inc(x_added[s], 1)

            pool_rstd(s, n, 0)
            yield
            pool_rstd(s, n, 1)
            yield
            difference(0)
            yield
            square_k(0)
            yield
            difference(1)
            yield
            add(0)
            yield
            square_k(1)
            yield
            yield
            add(1)
            yield

        def pool_proj3(n):
            pool_rstd("proj3", n, 0)
            yield
            pool_rstd("proj3", n, 1)
            yield
            yield
            for j in range(8):
                nc.gpsimd.wait_ge(mid_done, 8 * n + j + 1)
                nc.gpsimd.tensor_tensor(parts[:, j % 2, LO, :], x32[:, j % 2, :], parts[:, j % 2, MID, :],
                                        ALU.subtract).then_inc(lo_done, 1)
                yield

        def sp_att1(n):
            for h in range(2):
                nc.sync.wait_ge(xb_copied, 16 * n)
                nc.sync.wait_ge(xh_ready["proj3"], 2 * n)
                nc.sync.dma_start(xa[:, TPH * h:TPH * (h + 1), :],
                                  x_tok[n][:, TPH * h:TPH * (h + 1), :]).then_inc(x_loaded[h], 16)
            for _ in range(N_ATT1):
                yield

        def sp_proj3(n):
            for _ in range(3):
                yield
            for j in range(8):
                h, kq, ht = j // 4, (j // NHT) % 2, j % NHT
                nc.sync.wait_ge(lo_done, 8 * n + j + 1)
                nc.sync.dma_start(
                    parts_dram[n, kq, ht].rearrange("r d h n -> (d h) r n")[:, :, HALF * h:HALF * (h + 1)],
                    parts[:, j % 2, :, :]).then_inc(part_stored[j % 2], 16)
                yield

        def sp_copy(n):
            nc.sync.wait_ge(x_added["ffn2"], 2 * n + 2)
            nc.sync.wait_ge(out_stored, 16 * n)
            nc.sync.dma_start(xb[:, :, :], xa[:, :, :]).then_inc(xb_copied, 16)

        def sp_store(n):
            nc.sync.wait_ge(x_added["ffn4"], 2 * n + 2)
            nc.sync.dma_start(out_tok[n], xb[:, :, :]).then_inc(out_stored, 16)

        def sp_stack(n, g):
            r = STACK_OF[g]
            ht, h0 = g // 2, GH * (g % 2)
            nc.sync.wait_ge(s_full, GH * NP * (NG * n + (1 if g == 3 else 0)))
            for k in range(2):
                nc.sync.wait_ge(part_stored[k], 64 * n + 64)
            src = parts_dram[n]

            def copy(to, kq, slot, part, count):
                nc.sync.dma_start(
                    to[HD * slot:HD * (slot + count), :, :],
                    src[kq, ht, part:part + count].rearrange("r d h n -> (r d) h n")[:, h0:h0 + GH, :]
                ).then_inc(stack_ready[r], 16)

            copy(ks[r], 0, 0, HI, 3)
            copy(ks[r], 0, 3, HI, 2)
            copy(ks[r], 0, 5, HI, 1)
            for slot, part in enumerate(Q_SLOTS):
                copy(qs[r], 1, slot, part, 1)

        emptied = [None, None]

        def side_job(k, taken, value):
            if emptied[k] is not None:
                nc.tensor.wait_ge(*emptied[k])
            emptied[k] = (taken, value)
            return side[k]

        def pe_transposed(s, src, n, h):
            nc.tensor.wait_ge(xh_ready[s], 2 * n + h + 1)
            for c in range(NC):
                bank = side_job(c, xt_ready[s], 4 * n + 2 * h + c + 1)
                for t in range(TPH):
                    mm = nc.tensor.transpose(bank[:, P * t:P * (t + 1)], src[:, t, P * c:P * (c + 1)],
                                             ident[:, :])
                mm.then_inc(tr_full[s], 1)

        def pe_att1(n):
            pe = nc.tensor

            def values(t):
                if t % TPH == 0:
                    pe.wait_ge(xt_ready["att1"], 4 * n + 2 * (t // TPH) + 2)
                bank = side_job(t % 2, vp_ready, 8 * n + t + 1)
                for c in range(NC):
                    mm = pe.matmul(bank[:, 0:C + 3], xta[:, c, P * t:P * (t + 1)], wvp[:, c, :],
                                   start=(c == 0), stop=(c == NC - 1))
                mm.then_inc(v1_full, 1)

            def positions(c, h):
                pe.wait_ge(vp_ready, 8 * n + TPH * (h + 1))
                bank = side_job((3 * h + c) % 2, pb_ready, 6 * n + 3 * h + c + 1)
                for t in range(TPH):
                    mm = pe.transpose(bank[:, P * t:P * (t + 1)],
                                      vp[:, TPH * h + t, POS + c:POS + c + 1].to_broadcast([P, P]),
                                      ident[:, :])
                mm.then_inc(pb_full, 1)

            def attend(t):
                m = t + 1 if t < TPH else TPH + t + 1
                pe.wait_ge(p1_exp, NP * n + m)
                pe.wait_ge(p1_sel, NT * n + t + 1)
                bank = side_job(t % 2, x1_done, 8 * n + t + 1)
                for kt in range(t + 1):
                    at = P1_AT[kt] + P * (t - kt)
                    mm = pe.matmul(bank[:, 0:VC], p1[:, at:at + P], vp[:, kt, :],
                                   start=(kt == 0), stop=(kt == t))
                mm.then_inc(pv1_full, 1)

            yield
            pe_transposed("att1", xha, n, 0)
            yield
            pe_transposed("att1", xha, n, 1)
            values(0)
            values(1)
            yield
            values(2)
            values(3)
            yield
            values(4)
            values(5)
            positions(0, 0)
            yield
            values(6)
            values(7)
            positions(1, 0)
            yield
            positions(2, 0)
            positions(0, 1)
            yield
            positions(1, 1)
            positions(2, 1)
            yield
            for p in range(NP + 2):
                if 2 <= p < 2 + TPH:
                    attend(p - 2)
                if 2 + 2 * TPH <= p < 2 + 3 * TPH:
                    attend(p - 2 - TPH)
                yield

        def pe_ffn(s, n):
            pe = nc.tensor

            def keys(h):
                pe.wait_ge(xk_ready[s], 2 * n + h + 1)
                for j in range(2):
                    bank = side_job(j, kr_ready[s], 4 * n + 2 * h + j + 1)
                    for c in range(NC):
                        mm = pe.matmul(bank[:, :], wkT[:, c, P * j:P * (j + 1)], xk[:, c, :],
                                       start=(c == 0), stop=(c == NC - 1))
                    mm.then_inc(k_full[s], 1)

            def pair(h, lhs, rhs, full, taken):
                for j in range(2):
                    bank = side_job(j, taken, 4 * n + 2 * h + j + 1)
                    for t in range(2):
                        at = P * (2 * j + t)
                        for c in range(NC):
                            mm = pe.matmul(bank[:, C * t:C * (t + 1)], lhs[:, c, at:at + P], rhs[:, c, :],
                                           start=(c == 0), stop=(c == NC - 1))
                    mm.then_inc(full, 1)

            def receptance(h):
                pe.wait_ge(xr_ready[s], 2 * n + h + 1)
                pair(h, xr, wrT, r_full[s], rexp_done[s])

            def values(h):
                pe.wait_ge(ka_ready[s], 4 * n + 2 * h + 2)
                pair(h, ka, wvT, v_full[s], tm_ready[s])

            yield
            pe_transposed(s, xhb, n, 0)
            yield
            pe_transposed(s, xhb, n, 1)
            yield
            keys(0)
            yield
            receptance(0)
            yield
            values(0)
            yield
            keys(1)
            yield
            receptance(1)
            yield
            values(1)
            yield

        def pe_proj3(n):
            pe = nc.tensor
            yield
            pe_transposed("proj3", xha, n, 0)
            yield
            pe_transposed("proj3", xha, n, 1)
            yield
            for j in range(8):
                h, kq, ht = j // 4, (j // NHT) % 2, j % NHT
                pe.wait_ge(xt_ready["proj3"], 4 * n + 2 * h + 2)
                bank = side_job(j % 2, x32_ready, 8 * n + j + 1)
                for c in range(NC):
                    mm = pe.matmul(bank[:, :], wkq[:, c, kq, ht, :, :], xta[:, c, HALF * h:HALF * (h + 1)],
                                   start=(c == 0), stop=(c == NC - 1))
                mm.then_inc(kq_full, 1)
                yield

        def pe_values3(n):
            for j in range(4):
                bank = side_job(j % 2, v3_ready, 4 * n + j + 1)
                for t in range(2):
                    at = P * (2 * j + t)
                    for c in range(NC):
                        mm = nc.tensor.matmul(bank[:, C * t:C * (t + 1)], xta[:, c, at:at + P],
                                              wv3[:, c, :, :], start=(c == 0), stop=(c == NC - 1))
                mm.then_inc(v3_full, 1)
            yield

        def pe_att3(i, t):
            pe = nc.tensor
            if t < NG * NP:
                g, m = divmod(t, NP)
                tile, k0, k1 = QUERY_PIECES[m]
                r = STACK_OF[g]
                if m == 0:
                    pe.wait_ge(stack_ready[r], 16 * N_STACK_DMA * (STACK_LOADS[r] * i + STACK_NTH[g] + 1))
                for j in range(GH):
                    k = GH * t + j
                    pe.wait_ge(max_free, GH * NG * NP * i + max(0, k - 1))
                    pe.matmul(max_bank[k % 2][:, 0:k1 - k0], qs[r][0:KROWS, j, P * tile:P * (tile + 1)],
                              ks[r][0:KROWS, j, k0:k1], start=True, stop=True).then_inc(max_full, 1)
            if t >= NP + 1 and (t - NP - 1) % NP == 0 and (t - NP - 1) // NP < NG:
                g = (t - NP - 1) // NP
                pe.wait_ge(negmax_ready, NG * i + g + 1)
                bank = side_job(g % 2, negmaxT_ready, NG * i + g + 1)[:, :].bitcast(BF16)
                for c in range(2):
                    mm = pe.transpose(bank[0:GH * NT, P * c:P * (c + 1)],
                                      neg_max[:, c, :, :].rearrange("p j t -> p (j t)"), identb[:, :])
                mm.then_inc(negmaxT_full, 1)
            e = t - LEAD
            if 0 <= e < NG * NP:
                g, m = divmod(e, NP)
                kt, q0, q1 = KEY_PIECES[m]
                r = STACK_OF[g]
                if m == 0:
                    pe.wait_ge(crow_ready, 32 * (NG * i + g + 1))
                for j in range(GH):
                    k = GH * e + j
                    pe.wait_ge(exp_done, GH * NG * NP * i + max(0, k - 1))
                    mm = pe.matmul(exp_bank[k % 2][:, 0:q1 - q0], ks[r][:, j, P * kt:P * (kt + 1)],
                                   qs[r][:, j, q0:q1], start=True, stop=True).then_inc(s_full, 1)
            if 1 <= e <= NG * NP:
                g, m = divmod(e - 1, NP)
                kt, q0, q1 = KEY_PIECES[m]
                h = 0 if m < TPH else 1
                pe.wait_ge(exp_done, GH * (NG * NP * i + e))
                if DIAGONAL[m]:
                    pe.wait_ge(sel_done, NG * NT * i + NT * g + NTH_DIAGONAL[m] + 1)
                if kt == 0:
                    pe.wait_ge(ot_ready, 8 * i + max(0, 2 * g + h - 1))
                for j in range(GH):
                    mm = pe.matmul(o_bank[h][32 * j:32 * j + VW, q0 - HALF * h:q1 - HALF * h],
                                   v3[:, kt, GH * g + j, :], pt[:, (e - 1) % 2, j, 0:q1 - q0],
                                   start=(kt == 0), stop=(q1 - q0 == P), skip_group_check=True)
                mm.then_inc(pv_done, 1)
            for h, at in ((0, 7), (1, NP + 3)):
                if e >= at and (e - at) % NP == 0 and (e - at) // NP < NG:
                    g = (e - at) // NP
                    pe.wait_ge(ot_ready, 8 * i + 2 * g + h + 1)
                    bank = side_job(h, on_ready, 8 * i + 2 * g + h + 1)
                    for q in range(TPH):
                        mm = pe.transpose(bank[:, P * q:P * (q + 1)], ot[:, h, P * q:P * (q + 1)], ident[:, :])
                    mm.then_inc(on_full, 1)

        def act_att3(i, t):
            act = nc.scalar
            e = t - LEAD
            if 0 <= e < NG * NP:
                m = e % NP
                kt, q0, q1 = KEY_PIECES[m]
                act.wait_ge(pv_done, NG * NP * i + max(0, e - 1))
                for j in range(GH):
                    k = GH * e + j
                    act.wait_ge(s_full, GH * NG * NP * i + k + 1)
                    act.activation(pt[:, e % 2, j, 0:q1 - q0], exp_bank[k % 2][:, 0:q1 - q0], ACT.Exp,
                                   scale=SCALE).then_inc(exp_done, 1)
            for h, at in ((0, 5), (1, NP + 1)):
                if e >= at and (e - at) % NP == 0 and (e - at) // NP < NG:
                    g = (e - at) // NP
                    act.wait_ge(pv_done, NG * NP * i + NP * g + (TPH if h == 0 else NP))
                    act.wait_ge(on_full, 8 * i + max(0, 2 * g + h - 1))
                    act.activation(ot[:, h, :], o_bank[h][:, :], ACT.Copy).then_inc(ot_ready, 1)

        def dve_att3(i, t):
            dve = nc.vector
            if t < NG * NP:
                g, m = divmod(t, NP)
                tile, k0, k1 = QUERY_PIECES[m]
                w = k1 - k0
                if m == 0:
                    dve.wait_ge(negmax_ready, NG * i + g)
                for j in range(GH):
                    k = GH * t + j
                    dve.wait_ge(max_full, GH * NG * NP * i + k + 1).then_inc(scores_seen, 1)
                    if k1 == P * (tile + 1):
                        dve.tensor_tensor_reduce(max_bank[k % 2][:, 0:w], max_bank[k % 2][:, 0:w],
                                                 mask[:, HALF - w:HALF], 1.0, LOWEST, ALU.add, ALU.max,
                                                 piece_max[:, j, m:m + 1]).then_inc(max_free, 1)
                    else:
                        dve.tensor_reduce(piece_max[:, j, m:m + 1], max_bank[k % 2][:, 0:w], AX.X,
                                          ALU.max).then_inc(max_free, 1)
                if m == NP - 1:
                    base = 2 * (NG * i + g)
                    dve.wait_ge(max_free, GH * (NG * NP * i + t + 1))
                    dve.tensor_tensor(piece_max[:, :, TPH:NT], piece_max[:, :, TPH:NT],
                                      piece_max[:, :, NT:NP], ALU.max).then_inc(c_step, 1)
                    dve.wait_ge(c_step, base + 1)
                    dve.tensor_scalar(neg_max[:, 0, :, :], piece_max[:, :, 0:NT], -1.0, None,
                                      ALU.mult).then_inc(c_step, 1)
                    dve.wait_ge(c_step, base + 2)
                    dve.scalar_tensor_tensor(out=neg_max[:, 1, :, :], in0=piece_max[:, :, 0:NT],
                                             scalar=-1.0, in1=neg_max[:, 0, :, :], op0=ALU.mult,
                                             op1=ALU.subtract).then_inc(negmax_ready, 1)
            if t >= NP + 1 and (t - NP - 1) % NP == 0 and (t - NP - 1) // NP < NG:
                g = (t - NP - 1) // NP
                dve.wait_ge(negmaxT_full, NG * i + g + 1)
                dve.wait_ge(crow_ready, 32 * (NG * i + g))
                bank = side[g % 2][:, :].bitcast(BF16)
                dve.tensor_copy(neg_maxT[:, :, :],
                                bank[0:GH * NT, 0:2 * P].rearrange("p (c n) -> p c n", c=2)
                                ).then_inc(negmaxT_ready, 1)
            e = t - LEAD
            for h, at in ((0, 7), (1, NP + 3)):
                if e >= at and (e - at) % NP == 0 and (e - at) // NP < NG:
                    g = (e - at) // NP
                    n = 8 * i + 2 * g + h
                    dve.wait_ge(on_full, n + 1)
                    o = side[h][:, :].rearrange("p (t j d) -> p t j d", t=TPH, j=GH)
                    dve.wait_ge(on_ready, n)
                    dve.reciprocal(rsum[:, :, :], o[:, :, :, HD]).then_inc(rsum_done, 1)
                    dve.wait_ge(rsum_done, n + 1)
                    dve.wait_ge(xb_added, n)
                    dve.tensor_tensor(on[:, :, :, :], o[:, :, :, 0:HD],
                                      rsum[:, :, :].unsqueeze(3).to_broadcast([P, TPH, GH, HD]),
                                      ALU.mult).then_inc(on_ready, 1)

        def pool_att3(i, t):
            pool = nc.gpsimd
            e = t - LEAD
            if 0 <= e < NG * NP and DIAGONAL[e % NP]:
                block = pt[:, e % 2, :, 0:P]
                pool.wait_ge(exp_done, GH * (NG * NP * i + e + 1)).then_inc(exp_seen, 1)
                pool.affine_select(out=block, in_=block, compare_op=ALU.is_ge, fill=0.0, base=0,
                                   pattern=[[0, GH], [1, P]], channel_multiplier=-1).then_inc(sel_done, 1)
            for h, at in ((0, 7), (1, NP + 3)):
                if e >= at and (e - at) % NP == 0 and (e - at) // NP < NG:
                    g = (e - at) // NP
                    pool.wait_ge(on_ready, 8 * i + 2 * g + h + 1)
                    pool.wait_ge(xb_copied, 16 * i + 16)
                    x_half = xb[:, TPH * h:TPH * (h + 1), GH * HD * g:GH * HD * (g + 1)]
                    pool.tensor_tensor(x_half, x_half, on[:, :, :, :].rearrange("p t j d -> p t (j d)"),
                                       ALU.add).then_inc(xb_added, 1)

        def sp_att3(i, t):
            if t >= NP + 1 and (t - NP - 1) % NP == 0 and (t - NP - 1) // NP < NG:
                g = (t - NP - 1) // NP
                r = STACK_OF[g]
                nc.sync.wait_ge(negmaxT_ready, NG * i + g + 1)
                for c in range(2):
                    nc.sync.dma_start(qs[r][KROWS + c:KROWS + c + 1, :, :], neg_maxT[:, c, :]
                                      ).then_inc(crow_ready, 16)
            if t == LEAD + NP:
                sp_stack(i, 3)

        def chain(*stages):
            for stage in stages:
                yield from stage

        def run(chunks):
            for _ in chunks:
                pass

        def attend_with(att, i, chunks, count, slots=SLOTS - 1):
            done = 0
            for t in range(SLOTS):
                att(i, t)
                while done < min(count, count * (t + 1) // slots):
                    next(chunks)
                    done += 1

        N_ATT1, N_FFN, N_PROJ3 = 8 + NP + 2, 9, 11
        N_BEFORE = N_ATT1 + N_FFN + N_PROJ3

        def schedule(eng, att, before, first, ffn4, last, enter=lambda n: None):
            run(before(0))
            run(first(0))
            attend_with(att, 0, before(1), N_BEFORE)
            run(first(1))
            with eng.Fori(0, B - 2) as r:
                enter(r + 1)
                attend_with(att, r + 1, chain(ffn4(r), last(r), before(r + 2)), N_FFN + 1 + N_BEFORE)
                run(first(r + 2))
            enter(B - 1)
            attend_with(att, B - 1, chain(ffn4(B - 2), last(B - 2)), N_FFN + 1, NP + 4)
            run(ffn4(B - 1))
            run(last(B - 1))

        def nothing(n):
            yield

        def no_ffn(n):
            for _ in range(N_FFN):
                yield

        block = ctx.enter_context(nc.Block())

        @block.sync
        def _(sp):
            for k, w in enumerate((wv, wo, w_r, w_k, w_v)):
                sp.dma_start(raw[:, k, :, :], w.rearrange("(a p) c -> p a c", p=P)).then_inc(raw_loaded, 16)
            sp.dma_start(raw3d, w3d).then_inc(raw_loaded, 16)
            for a in range(NC):
                sp.dma_start(raw_kqv[:, a, :, :],
                             wkqv[:, P * a:P * (a + 1), :].rearrange("h c f -> c h f")).then_inc(raw_loaded, 16)
            for row, v in ((bv_row, bv), (mur_row, mu_r), (muk_row, mu_k)):
                sp.dma_start(row, v.rearrange("(a n) -> a n", a=1)).then_inc(rows_loaded, 16)
            sp.dma_start(rows[:, 3 * C:3 * C + H * 48],
                         bkqv.rearrange("(a h) f -> a (h f)", a=1)).then_inc(rows_loaded, 16)
            sp.dma_start(bo_all, bo.rearrange("(a n) -> a n", a=1).to_broadcast([P, C])).then_inc(rows_loaded, 16)
            sp.dma_start(bias_vp[:, C:C + 3],
                         b3d.rearrange("(a n) -> a n", a=1).to_broadcast([P, 3])).then_inc(rows_loaded, 16)
            sp.dma_start(bv3[:, :, :], bkqv[:, 2 * HD:3 * HD].unsqueeze(0).to_broadcast([P, H, HD])
                         ).then_inc(rows_loaded, 16)

            def before(n):
                return chain(sp_att1(n), no_ffn(n), sp_proj3(n))

            def first(n):
                if isinstance(n, int) and n == 0:
                    sp_copy(0)
                for g in range(3):
                    sp_stack(n, g)
                yield

            def last(n):
                sp_store(n)
                if not (isinstance(n, int) and n == B - 1):
                    sp_copy(n + 1)
                yield

            schedule(sp, sp_att3, before, first, no_ffn, last)
            sp.wait_ge(out_stored, 16 * B)

        @block.gpsimd
        def _(pool):
            pool.memset(ident[:, :], 0.0).then_inc(cleared, 1)
            pool.memset(identb[:, :], 0.0).then_inc(cleared, 1)
            pool.memset(mask[:, :], 0.0).then_inc(cleared, 1)
            pool.wait_ge(cleared, 3)
            for m in (ident, identb):
                pool.affine_select(out=m[:, :], in_=m[:, :], compare_op=ALU.not_equal, fill=1.0, base=0,
                                   pattern=[[-1, P]], channel_multiplier=1).then_inc(consts_ready, 1)
            tail = mask[:, HALF - P:HALF]
            pool.affine_select(out=tail, in_=tail, compare_op=ALU.is_ge, fill=LOWEST, base=0,
                               pattern=[[-1, P]], channel_multiplier=1).then_inc(consts_ready, 1)
            pool.memset(minus_half[:, :], -0.5).then_inc(consts_ready, 1)
            pool.memset(xtb[:, :, 0:1], 0.0).then_inc(consts_ready, 1)
            pool.memset(vp[:, :, ONE:ONE + 1], 1.0).then_inc(consts_ready, 1)
            pool.memset(v3[:, :, :, HD:VW], 1.0).then_inc(consts_ready, 1)
            pool.wait_ge(consts_ready, 7)
            for r in range(STACKS):
                pool.memset(ks[r][KROWS:SROWS, :, :], 1.0).then_inc(consts_ready, 1)

            def before(n):
                return chain(pool_att1(n), pool_ffn("ffn2", xa, n), pool_proj3(n))

            pool.wait_ge(consts_ready, 7 + STACKS)
            pool.wait_ge(weights_ready, 1)
            schedule(pool, pool_att3, before, nothing, lambda n: pool_ffn("ffn4", xb, n), nothing)

        @block.scalar
        def _(act):
            def before(n):
                return chain(act_att1(n), act_ffn("ffn2", n), act_proj3(n))

            act.preload_act_table_set("natural_log_exp_and_others")
            act.wait_ge(weights_ready, 1)
            schedule(act, act_att3, before, nothing, lambda n: act_ffn("ffn4", n), nothing)

        @block.vector
        def _(dve):
            for k in range(2):
                dve.memset(o_bank[k][:, :], 0.0)
            dve.wait_ge(raw_loaded, 16 * 8)
            dve.wait_ge(rows_loaded, 16 * 7)
            for q in range(2):
                dve.tensor_copy(bkq_row[:, q, :, :, :],
                                kqv_row[:, :, :, HD * q:HD * (q + 1)].rearrange("p t h d -> p t d h")
                                ).then_inc(rows_ready, 1)
            kqv = raw_kqv.rearrange("p a (t h) f -> p a t h f", t=NHT)
            for a in range(NC):
                for q in range(2):
                    for t in range(NHT):
                        dve.tensor_copy(wkq[:, a, q, t, :, :],
                                        kqv[:, a, t, :, HD * q:HD * (q + 1)].rearrange("p h d -> p d h"))
            dve.tensor_copy(wv3[:, :, :, :], raw_kqv[:, :, :, 2 * HD:3 * HD])
            job = 0
            for dst in (wvp, wrT, wkT, wvT):
                for a in range(NC):
                    dve.wait_ge(setup_full, job + 1)
                    dve.tensor_copy(dst[:, a, 0:C], side[job % 2][:, 0:C]).then_inc(setup_taken, 1)
                    job += 1
            dve.wait_ge(setup_full, job + 1)
            dve.tensor_copy(cols[:, :], side[job % 2][:, 0:10]).then_inc(setup_taken, 1)
            job += 1
            dve.memset(bv_wide, 1.0).then_inc(bv_spread, 1)
            dve.wait_ge(setup_taken, job)
            dve.wait_ge(bv_spread, 1)
            for a in range(NC):
                dve.tensor_scalar(bv_wide[:, a, :], bv_wide[:, a, :], cols[:, BV + a:BV + a + 1], None,
                                  ALU.mult).then_inc(bv_spread, 1)
            dve.wait_ge(setup_full, job + 1)
            dve.tensor_copy(wvp[:, :, C:C + 3],
                            side[job % 2][:, 0:3 * NC].rearrange("p (a k) -> p a k", a=NC)
                            ).then_inc(setup_taken, 1)
            job += 1
            dve.wait_ge(setup_full, job + 1)
            dve.tensor_tensor(bias_vp[:, 0:C], side[job % 2][:, 0:C], bo_all, ALU.add).then_inc(setup_taken, 1)
            job += 1
            dve.wait_ge(setup_full, job + 2)
            for a in range(NC):
                dve.tensor_copy(wvp[:, a, 0:C], side[job % 2][:, 0:C]).then_inc(setup_taken, 1)
                job += 1
            dve.memset(rinv1[:, :], 0.0).then_inc(weights_ready, 1)
            dve.wait_ge(weights_ready, 1)
            dve.wait_ge(consts_ready, 7 + STACKS)

            def before_ffn2(n):
                if isinstance(n, int) and n < 2:
                    return x_added["ffn2"], 2 * n
                return x_added["ffn4"], 2 * (n - 1)

            def before_ffn4(n):
                if isinstance(n, int) and n == B - 1:
                    return x_added["ffn4"], 2 * n
                return x_added["ffn2"], 2 * (n + 2)

            def before(n):
                return chain(dve_att1(n), dve_ffn("ffn2", xa, n, before_ffn2(n)), dve_proj3(n))

            schedule(dve, dve_att3, before, dve_values3, lambda n: dve_ffn("ffn4", xb, n, before_ffn4(n)), nothing)

        @block.tensor
        def _(pe):
            pe.wait_ge(consts_ready, 7 + STACKS)
            pe.wait_ge(raw_loaded, 16 * 8)
            pe.wait_ge(rows_loaded, 16 * 7)
            pe.wait_ge(rows_ready, 2)
            jobs = [0]

            def setup_job():
                jobs[0] += 1
                return side_job((jobs[0] - 1) % 2, setup_taken, jobs[0])

            for k in (1, 2, 3, 4):
                for c in range(NC):
                    bank = setup_job()
                    for a in range(NC):
                        mm = pe.transpose(bank[:, P * a:P * (a + 1)], raw[:, k, a, P * c:P * (c + 1)], ident[:, :])
                    mm.then_inc(setup_full, 1)
            bank = setup_job()
            pieces = [row[:, P * a:P * (a + 1)] for row in (bv_row, mur_row, muk_row) for a in range(NC)]
            pieces += [bkq_row[:, q, t, :, :] for q in range(2) for t in range(NHT)]
            for k, piece in enumerate(pieces):
                mm = pe.matmul(bank[:, k:k + 1], piece, ident[0:1, 0:1], start=True, stop=True)
            mm.then_inc(setup_full, 1)
            bank = setup_job()
            for a in range(NC):
                mm = pe.transpose(bank[:, 3 * a:3 * (a + 1)], raw3d[:, P * a:P * (a + 1)], ident[0:3, 0:3])
            mm.then_inc(setup_full, 1)
            pe.wait_ge(bv_spread, 3)
            bank = setup_job()
            for a in range(NC):
                mm = pe.matmul(bank[:, 0:C], bv_wide[:, a, :], wvp[:, a, 0:C], start=(a == 0), stop=(a == NC - 1))
            mm.then_inc(setup_full, 1)
            for c in range(NC):
                bank = setup_job()
                for a in range(NC):
                    mm = pe.matmul(bank[:, 0:C], raw[:, 0, a, P * c:P * (c + 1)], wvp[:, a, 0:C],
                                   start=(a == 0), stop=(a == NC - 1))
                mm.then_inc(setup_full, 1)
            pe.wait_ge(weights_ready, 1)

            def enter(n):
                for k in range(2):
                    emptied[k] = (v3_ready, 4 * n + 3 + k)

            def before(n):
                return chain(pe_att1(n), pe_ffn("ffn2", n), pe_proj3(n))

            schedule(pe, pe_att3, before, pe_values3, lambda n: pe_ffn("ffn4", n), nothing, enter)


_INS = ['L0_attn_a_x', 'L0_attn_a_wq', 'L0_attn_a_bq', 'L0_attn_a_wk', 'L0_attn_a_bk', 'L0_attn_a_wv',
        'L0_attn_a_bv', 'L0_attn_a_wo', 'L0_attn_a_bo', 'L0_attn_a_w3d', 'L0_attn_a_b3d',
        'L0_attn_b_Wkqv', 'L0_attn_b_bkqv', 'L0_ffn_W_r', 'L0_ffn_W_k', 'L0_ffn_W_v', 'L0_ffn_mu_r',
        'L0_ffn_mu_k']
_OUTS = [((B, S, C), 'float32')]


def kernel(**inputs):
    import numpy as _np
    import concourse.bacc as _bacc
    from concourse import mybir as _mybir
    from concourse.bass_utils import run_bass_kernel_spmd as _run

    nc = _bacc.Bacc("TRN2", target_bir_lowering=False, num_devices=1)
    arrays, args = {}, []
    for name in _INS:
        a = _np.ascontiguousarray(inputs[name])
        arrays[f"in_{name}_dram"] = a
        args.append(nc.dram_tensor(f"in_{name}_dram", a.shape, _mybir.dt.from_np(a.dtype), kind="ExternalInput").ap())
    for i, (shape, dtype) in enumerate(_OUTS):
        dt = _mybir.dt.from_np(_np.dtype(dtype))
        args.append(nc.dram_tensor(f"out_{i}_dram", shape, dt, kind="ExternalOutput").ap())
    bass_hybrid(nc, *args)
    r = _run(nc, [arrays], core_ids=[0])
    return r.results[0]["out_0_dram"]
```

```python
from contextlib import ExitStack

import concourse.bass as bass
from concourse import mybir

F32 = mybir.dt.float32
BF16 = mybir.dt.bfloat16
ALU = mybir.AluOpType
ACT = mybir.ActivationFunctionType
AX = mybir.AxisListType

P = 128
B, S, C = 8, 1024, 256
H, HD = 16, 16
NT = S // P
NC = C // P
HALF = S // 2
TPH = HALF // P
GH = 4
NG = H // GH
H8 = P // HD
NHT = H // H8
EPS = 1e-5
SCALE = HD ** -0.5
TINY = 1e-30
LOWEST = -3.0e38
VC = C + 4
POS, ONE = C, C + 3
VW = HD + 1

HI, MID, LO = 0, 1, 2
K_SLOTS = (HI, MID, LO, HI, MID, HI)
Q_SLOTS = (HI, HI, HI, MID, MID, LO)
KROWS = HD * len(K_SLOTS)
SROWS = KROWS + 2
STACKS = 3
STACK_OF = (0, 1, 2, 0)
STACK_LOADS = (2, 1, 1)
STACK_NTH = (0, 0, 0, 1)
N_STACK_DMA = 9

KEY_PIECES = [(kt, P * kt, HALF) for kt in range(TPH)] + \
             [(kt, max(HALF, P * kt), S) for kt in range(NT)]
DIAGONAL = [q0 == P * kt for kt, q0, _ in KEY_PIECES]
NTH_DIAGONAL = [sum(DIAGONAL[:m]) for m in range(len(KEY_PIECES))]
QUERY_PIECES = [(i, 0, P * (i + 1)) for i in range(TPH)] + \
               [(i, 0, HALF) for i in range(TPH, NT)] + \
               [(i, HALF, P * (i + 1)) for i in range(TPH, NT)]
NP = len(KEY_PIECES)
assert NP == len(QUERY_PIECES) == 12
LEAD = NP + 3
SLOTS = NG * NP + LEAD + 4
DENSE = 2 * LEAD
LAST_SIDE = 2 * (NG * NP + NP)
P1_AT = [sum(S - P * j for j in range(kt)) for kt in range(NT)]
P1_COLS = sum(S - P * j for j in range(NT))


def bass_hybrid(nc, x, wq, bq, wk, bk, wv, bv, wo, bo, w3d, b3d, wkqv, bkqv, w_r, w_k, w_v,
                mu_r, mu_k, out):
    parts_dram = nc.dram_tensor("parts_dram", [B, 2, NHT, 3, HD, H8, S], BF16, kind="Internal").ap()

    nc.disable_value_cache = True

    with ExitStack() as ctx:
        def sb(name, shape, dt=F32):
            return ctx.enter_context(nc.sbuf_tensor(name, shape, dt))

        def psum(name):
            return ctx.enter_context(nc.psum_tensor(name, [P, HALF], F32))

        def sem(name):
            return ctx.enter_context(nc.semaphore(name))

        side = [psum(f"side{k}") for k in range(2)]
        max_bank = [psum(f"max_bank{k}") for k in range(2)]
        exp_bank = [psum(f"exp_bank{k}") for k in range(2)]
        o_bank = [psum(f"o_bank{k}") for k in range(2)]

        ident = sb("ident", [P, P])
        identb = sb("identb", [P, P], BF16)
        mask = sb("mask", [P, HALF])
        wvp = sb("wvp", [P, NC, C + 3])
        bias_vp = sb("bias_vp", [P, C + 3])
        wrT = sb("wrT", [P, NC, C])
        wkT = sb("wkT", [P, NC, C])
        wvT = sb("wvT", [P, NC, C])                      
        wkq = sb("wkq", [P, NC, 2, NHT, HD, H8])
        wv3 = sb("wv3", [P, NC, H, HD])
        bv3 = sb("bv3", [P, H, HD])
        cols = sb("cols", [P, 10])
        BV, MUR, MUK, BKQ = 0, 2, 4, 6

        xa = sb("xa", [P, NT, C])
        xb = sb("xb", [P, NT, C])
        xha = sb("xha", [P, TPH, C])
        xhb = sb("xhb", [P, TPH, C])
        xta = sb("xta", [P, NC, S])
        xtb = sb("xtb", [P, NC, 1 + S])
        st = sb("st", [P, TPH, 6])
        mv = sb("mv", [P, TPH, 2])
        var_eps = sb("var_eps", [P, TPH])
        rstd = sb("rstd", [P, TPH])
        minus_half = sb("minus_half", [P, TPH])
        vp = sb("vp", [P, NT, VC])
        neg_pos = sb("neg_pos", [P, NT, 3])
        pb = sb("pb", [P, 3, S])
        sq = sb("sq", [P, 2, 3, HALF])
        p1 = sb("p1", [P, P1_COLS])
        rinv1 = sb("rinv1", [P, NT])
        xr, xk, ka = (pb[:, k, :].rearrange("p (c n) -> p c n", c=NC) for k in range(3))
        kr = sq[:, 0, 0:2, :]
        th = sq[:, 1, 0:2, :].rearrange("p a (b c) -> p (a b) c", c=C)
        tm = sb("tm", [P, TPH, C])
        x32 = sb("x32", [P, 2, HALF])
        parts = sb("parts", [P, 2, 3, HALF], BF16)
        v3 = sb("v3", [P, NT, H, VW])
        ks = [sb(f"ks{r}", [SROWS, GH, S], BF16) for r in range(STACKS)]
        qs = [sb(f"qs{r}", [SROWS, GH, S], BF16) for r in range(STACKS)]
        piece_max = sb("piece_max", [P, GH, NP])
        neg_max = sb("neg_max", [P, 2, GH, NT], BF16)
        neg_maxT = sb("neg_maxT", [GH * NT, 2, P], BF16)
        pt = sb("pt", [P, 2, GH, HALF])
        ot = sb("ot", [P, 2, HALF])
        rsum = sb("rsum", [P, TPH, GH])
        on = sb("on", [P, TPH, GH, HD])

        raw = pt[:, :, :, :].rearrange("p a b n -> p (a b n)")[:, 0:5 * NC * C].rearrange(
            "p (w a n) -> p w a n", w=5, a=NC)
        raw3d = ot[0:3, 0, 0:C]
        raw_kqv = p1[:, 0:NC * H * 48].rearrange("p (a h f) -> p a h f", a=NC, h=H)
        rows = sq[0:1, :, :, :].rearrange("p a b n -> p (a b n)")
        bv_row, mur_row, muk_row = (rows[:, k * C:(k + 1) * C] for k in range(3))
        kqv_row = rows[:, 3 * C:3 * C + H * 48].rearrange("p (t h f) -> p t h f", t=NHT, h=H8)
        bkq_row = rows[:, 3 * C + H * 48:3 * C + H * 48 + 2 * C].rearrange(
            "p (q t d h) -> p q t d h", q=2, t=NHT, d=HD)
        bo_all = tm[:, 0, :]
        bv_wide = tm[:, 1, :].rearrange("p (a n) -> p a n", a=NC)

        raw_loaded, rows_loaded, cleared, consts_ready, rows_ready, bv_spread, weights_ready = (
            sem(n) for n in ("raw_loaded", "rows_loaded", "cleared", "consts_ready", "rows_ready",
                             "bv_spread", "weights_ready"))
        setup_full, setup_taken = sem("setup_full"), sem("setup_taken")
        x_loaded = [sem(f"x_loaded{h}") for h in range(2)]
        xb_copied = [sem(f"xb_copied{h}") for h in range(2)]
        out_stored = [sem(f"out_stored{h}") for h in range(2)]
        STAGES = ("att1", "ffn2", "proj3", "ffn4")
        ln_step = {s: sem(f"{s}_ln_step") for s in STAGES}
        rstd_ready = {s: sem(f"{s}_rstd_ready") for s in STAGES}
        xh_ready = {s: sem(f"{s}_xh_ready") for s in STAGES}
        tr_full = {s: sem(f"{s}_tr_full") for s in STAGES}
        xt_ready = {s: sem(f"{s}_xt_ready") for s in STAGES}
        v1_full, vp_ready, neg_ready, pb_full, pb_ready = (
            sem(n) for n in ("v1_full", "vp_ready", "neg_ready", "pb_full", "pb_ready"))
        sq_ready, sum_ready, dist2_ready, log_done, dist_done, p1_exp, p1_sel, pv1_full, rinv_done, x1_done = (
            sem(n) for n in ("sq_ready", "sum_ready", "dist2_ready", "log_done", "dist_done", "p1_exp", "p1_sel",
                             "pv1_full", "rinv_done", "x1_done"))
        FF = ("ffn2", "ffn4")
        diff_done, xr_ready, xk_ready, k_full, r_full, kr_ready, ka_ready, rexp_done, rlog_done, th_ready, v_full, tm_ready, x_added = (
            {s: sem(f"{s}_{n}") for s in FF} for n in (
                "diff_done", "xr_ready", "xk_ready", "k_full", "r_full", "kr_ready", "ka_ready",
                "rexp_done", "rlog_done", "th_ready", "v_full", "tm_ready", "x_added"))
        kq_full, x32_ready, hi_done, rest_done, mid_done, lo_done, v3_full, v3_ready = (
            sem(n) for n in ("kq_full", "x32_ready", "hi_done", "rest_done", "mid_done", "lo_done",
                             "v3_full", "v3_ready"))
        part_stored = [sem(f"part_stored{k}") for k in range(2)]
        stack_ready = [sem(f"stack_ready{r}") for r in range(STACKS)]
        max_full, max_free, c_step, negmax_ready, negmaxT_full, negmaxT_ready, crow_ready = (
            sem(n) for n in ("max_full", "max_free", "c_step", "negmax_ready", "negmaxT_full",
                             "negmaxT_ready", "crow_ready"))
        s_full, exp_done, sel_done, pv_done, ot_ready, on_full, rsum_done, on_ready, xb_added = (
            sem(n) for n in ("s_full", "exp_done", "sel_done", "pv_done", "ot_ready",
                             "on_full", "rsum_done", "on_ready", "xb_added"))
        o_full = [sem(f"o_full{h}") for h in range(2)]
        third_ready = sem("third_ready")
        stats_seen, p1_seen, exp_seen, scores_seen = (
            sem(name) for name in ("stats_seen", "p1_seen", "exp_seen", "scores_seen"))

        x_tok = x.rearrange("b (t p) c -> b p t c", p=P)
        out_tok = out.rearrange("b (t p) c -> b p t c", p=P)


        def summed_after(p):
            return [t for t in range(NT) if (t if t < TPH else TPH + t) == p - 2]

        def dve_normalise(s, src, dst, n, ready):
            dve = nc.vector

            def statistics(h):
                base = 6 * n + 3 * h
                ready(h)
                for t in range(TPH):
                    last = dve.bn_stats(st[:, t, :], src[:, TPH * h + t, :])
                last.then_inc(ln_step[s], 1)
                dve.wait_ge(ln_step[s], base + 1).then_inc(stats_seen, 1)
                for t in range(TPH):
                    last = dve.bn_aggr(mv[:, t, :], st[:, t, :])
                last.then_inc(ln_step[s], 1)
                dve.wait_ge(ln_step[s], base + 2)
                dve.tensor_scalar(var_eps[:, :], mv[:, :, 1], EPS, None, ALU.add).then_inc(ln_step[s], 1)

            def apply(h):
                dve.wait_ge(rstd_ready[s], 2 * n + h + 1)
                if h == 1:
                    dve.wait_ge(tr_full[s], 4 * n + 2)
                for t in range(TPH):
                    last = dve.tensor_scalar(dst[:, t, :], src[:, TPH * h + t, :], mv[:, t, 0:1],
                                             rstd[:, t:t + 1], ALU.subtract, ALU.mult)
                last.then_inc(xh_ready[s], 1)

            statistics(0)
            yield
            apply(0)
            dve.wait_ge(xh_ready[s], 2 * n + 1)
            statistics(1)
            yield
            yield
            apply(1)
            yield

        def dve_att1(n):
            dve = nc.vector

            def loaded(h):
                dve.wait_ge(x_loaded[h], 16 * n + 16)

            def values(t):
                dve.wait_ge(v1_full, 8 * n + t + 1)
                dve.tensor_tensor(vp[:, t, 0:C + 3], side[t % 2][:, 0:C + 3], bias_vp[:, :],
                                  ALU.add).then_inc(vp_ready, 1)

            def negate(h):
                dve.wait_ge(vp_ready, 8 * n + TPH * (h + 1))
                dve.tensor_scalar(neg_pos[:, TPH * h:TPH * (h + 1), :],
                                  vp[:, TPH * h:TPH * (h + 1), POS:POS + 3], -1.0, None,
                                  ALU.mult).then_inc(neg_ready, 1)

            def distance(p):
                kt, q0, q1 = KEY_PIECES[p]
                w = q1 - q0
                dve.wait_ge(sum_ready, NP * n + p + 1)
                dve.wait_ge(third_ready, NP * n + p + 1)
                dve.scalar_tensor_tensor(out=sq[:, p % 2, 0, 0:w], in0=sq[:, p % 2, 0, 0:w],
                                         scalar=TINY, in1=sq[:, p % 2, 2, 0:w],
                                         op0=ALU.max, op1=ALU.add).then_inc(dist2_ready, 1)

            def residual(t):
                dve.wait_ge(pv1_full, 8 * n + t + 1)
                dve.reciprocal(rinv1[:, t:t + 1], side[t % 2][:, ONE:ONE + 1]).then_inc(rinv_done, 1)
                dve.wait_ge(rinv_done, 8 * n + t + 1)
                dve.scalar_tensor_tensor(out=xa[:, t, :], in0=side[t % 2][:, 0:C],
                                         scalar=rinv1[:, t:t + 1], in1=xa[:, t, :],
                                         op0=ALU.mult, op1=ALU.add).then_inc(x1_done, 1)

            yield from dve_normalise("att1", xa, xha, n, loaded)
            yield
            values(0)
            values(1)
            yield
            values(2)
            values(3)
            negate(0)
            yield
            values(4)
            values(5)
            yield
            values(6)
            values(7)
            negate(1)
            yield
            yield
            yield
            yield
            for p in range(NP + 2):
                yield
                for t in summed_after(p):
                    residual(t)
                yield
                if p < NP:
                    distance(p)
                yield

        def dve_ffn(s, src, n, previous):
            dve = nc.vector

            def ready(h):
                if s == "ffn2":
                    dve.wait_ge(x1_done, 8 * n + TPH * (h + 1))
                else:
                    dve.wait_ge(xb_added, 8 * n + 2 * (NG - 1) + h + 1)

            def mix(h):
                dve.wait_ge(diff_done[s], 2 * n + h + 1)
                if h == 1:
                    dve.wait_ge(r_full[s], 4 * n + 2)
                before = xtb[:, :, HALF * h:HALF * h + HALF]
                for dst, mu, done in ((xr, MUR, xr_ready), (xk, MUK, xk_ready)):
                    for c in range(NC):
                        last = dve.scalar_tensor_tensor(
                            out=dst[:, c, :], in0=xk[:, c, :], scalar=cols[:, mu + c:mu + c + 1],
                            in1=before[:, c, :], op0=ALU.mult, op1=ALU.add)
                    last.then_inc(done[s], 1)

            def gate(h, j):
                if j == 0 and h == 0:
                    dve.wait_ge(*previous)
                elif j == 0:
                    dve.wait_ge(x_added[s], 2 * n + 1)
                dve.wait_ge(th_ready[s], 4 * n + 2 * h + j + 1)
                dve.wait_ge(v_full[s], 4 * n + 2 * h + j + 1)
                dve.tensor_tensor(tm[:, 2 * j:2 * j + 2, :], th[:, 2 * j:2 * j + 2, :],
                                  side[j][:, :].rearrange("p (t c) -> p t c", c=C),
                                  ALU.mult).then_inc(tm_ready[s], 1)

            yield from dve_normalise(s, src, xhb, n, ready)
            mix(0)
            yield
            for _ in range(4):
                yield
            gate(0, 0)
            yield
            gate(0, 1)
            mix(1)
            yield
            for _ in range(4):
                yield
            gate(1, 0)
            yield
            gate(1, 1)
            yield

        def dve_proj3(n):
            dve = nc.vector

            def ready(h):
                dve.wait_ge(x_added["ffn2"], 2 * n + h + 1)

            def split(j):
                r = j % 2
                if j >= 2:
                    dve.wait_ge(part_stored[r], 64 * n + 16 * (j // 2))
                else:
                    dve.wait_ge(part_stored[r], 64 * n)
                dve.wait_ge(x32_ready, 8 * n + j + 1)
                dve.tensor_copy(parts[:, r, HI, :], x32[:, r, :]).then_inc(hi_done, 1)
                dve.wait_ge(hi_done, 8 * n + j + 1)
                dve.tensor_tensor(x32[:, r, :], x32[:, r, :], parts[:, r, HI, :],
                                  ALU.subtract).then_inc(rest_done, 1)
                dve.wait_ge(rest_done, 8 * n + j + 1)
                dve.tensor_copy(parts[:, r, MID, :], x32[:, r, :]).then_inc(mid_done, 1)

            yield from dve_normalise("proj3", xa, xha, n, ready)
            yield
            yield
            for j in range(8):
                split(j)
                yield
            yield

        def dve_values3(n):
            for j in range(4):
                nc.vector.wait_ge(v3_full, 4 * n + j + 1)
                for t in range(2):
                    last = nc.vector.tensor_tensor(
                        v3[:, 2 * j + t, :, 0:HD],
                        side[j % 2][:, C * t:C * (t + 1)].rearrange("p (h d) -> p h d", d=HD),
                        bv3[:, :, :], ALU.add)
                last.then_inc(v3_ready, 1)
            yield

        def act_transposed(s, dst, off, n, h):
            for c in range(NC):
                nc.scalar.wait_ge(tr_full[s], 4 * n + 2 * h + c + 1)
                nc.scalar.activation(dst[:, c, off + HALF * h:off + HALF * (h + 1)], side[c][:, :],
                                     ACT.Copy).then_inc(xt_ready[s], 1)

        def act_att1(n):
            act = nc.scalar

            def positions(c, h):
                k = 3 * h + c
                act.wait_ge(pb_full, 6 * n + k + 1)
                act.activation(pb[:, c, HALF * h:HALF * (h + 1)], side[k % 2][:, :],
                               ACT.Copy).then_inc(pb_ready, 1)

            def square(p, c):
                if p >= NP:
                    return
                kt, q0, q1 = KEY_PIECES[p]
                w = q1 - q0
                if c == 0:
                    act.wait_ge(neg_ready, 2 * n + kt // TPH + 1)
                    act.wait_ge(pb_ready, 6 * n + (3 if q1 <= HALF else 6))
                    act.wait_ge(p1_exp, NP * n + max(0, p - 1))
                mm = act.activation(sq[:, p % 2, c, 0:w], pb[:, c, q0:q1], ACT.Square,
                                    bias=neg_pos[:, kt, c:c + 1])
                if c == 1:
                    mm.then_inc(sq_ready, 1)
                if c == 2:
                    mm.then_inc(third_ready, 1)

            def transform(p, k):
                if not 0 <= p < NP:
                    return
                kt, q0, q1 = KEY_PIECES[p]
                w = q1 - q0
                d = sq[:, p % 2, 0, 0:w]
                at = P1_AT[kt] + q0 - P * kt
                if k == 0:
                    act.wait_ge(dist2_ready, NP * n + p + 1)
                    act.activation(d, d, ACT.Ln).then_inc(log_done, 1)
                elif k == 1:
                    act.wait_ge(log_done, NP * n + p + 1)
                    act.activation(d, d, ACT.Exp, scale=0.5).then_inc(dist_done, 1)
                else:
                    if p == 0:
                        act.wait_ge(pv1_full, 8 * n)
                    act.wait_ge(dist_done, NP * n + p + 1)
                    act.activation(p1[:, at:at + w], d, ACT.Exp, scale=-SCALE).then_inc(p1_exp, 1)

            yield
            yield
            act.wait_ge(v3_full, 4 * n)
            act_transposed("att1", xta, 0, n, 0)
            yield
            yield
            act_transposed("att1", xta, 0, n, 1)
            yield
            for _ in range(4):
                yield
            positions(0, 0)
            positions(1, 0)
            yield
            positions(2, 0)
            positions(0, 1)
            yield
            positions(1, 1)
            positions(2, 1)
            yield
            for p in range(NP + 2):
                square(p, 0)
                transform(p - 1, 0)
                square(p, 1)
                yield
                transform(p - 1, 1)
                square(p, 2)
                yield
                transform(p - 1, 2)
                yield

        def act_ffn(s, n):
            act = nc.scalar

            def relu_k(h, j):
                act.wait_ge(k_full[s], 4 * n + 2 * h + j + 1)
                if h == 1:
                    act.wait_ge(ka_ready[s], 4 * n + j + 1)
                act.activation(kr[:, j, :], side[j][:, :], ACT.Relu).then_inc(kr_ready[s], 1)

            def sigmoid(h, j, k):
                job = 4 * n + 2 * h + j + 1
                r = th[:, 2 * j:2 * j + 2, :]
                if k == 0:
                    if h == 1:
                        act.wait_ge(tm_ready[s], 4 * n + j + 1)
                    act.wait_ge(r_full[s], job)
                    act.activation(r, side[j][:, :].rearrange("p (t c) -> p t c", c=C),
                                   ACT.Exp, scale=-1.0).then_inc(rexp_done[s], 1)
                elif k == 1:
                    act.wait_ge(rexp_done[s], job)
                    act.activation(r, r, ACT.Ln, bias=1.0).then_inc(rlog_done[s], 1)
                else:
                    act.wait_ge(rlog_done[s], job)
                    act.activation(r, r, ACT.Exp, scale=-1.0).then_inc(th_ready[s], 1)

            yield
            yield
            act_transposed(s, xtb, 1, n, 0)
            yield
            yield
            act_transposed(s, xtb, 1, n, 1)
            yield
            for h in range(2):
                for j in range(2):
                    relu_k(h, j)
                    yield
                sigmoid(h, 0, 0)
                yield
                sigmoid(h, 1, 0)
                sigmoid(h, 0, 1)
                yield
                sigmoid(h, 0, 2)
                sigmoid(h, 1, 1)
                yield
                sigmoid(h, 1, 2)
                yield

        def act_proj3(n):
            act = nc.scalar
            yield
            yield
            act_transposed("proj3", xta, 0, n, 0)
            yield
            yield
            act_transposed("proj3", xta, 0, n, 1)
            yield
            for j in range(8):
                kq, ht = (j // NHT) % 2, j % NHT
                act.wait_ge(kq_full, 8 * n + j + 1)
                if j >= 2:
                    act.wait_ge(lo_done, 8 * n + j - 1)
                else:
                    act.wait_ge(lo_done, 8 * n)
                act.activation(x32[:, j % 2, :], side[j % 2][:, :], ACT.Identity,
                               bias=cols[:, BKQ + 2 * kq + ht:BKQ + 2 * kq + ht + 1]).then_inc(x32_ready, 1)
                yield
            yield
            yield

        def pool_rstd(s, n, h):
            nc.gpsimd.wait_ge(ln_step[s], 6 * n + 3 * h + 3)
            nc.gpsimd.tensor_tensor(rstd[:, :], var_eps[:, :], minus_half[:, :],
                                    ALU.pow).then_inc(rstd_ready[s], 1)

        def pool_att1(n):
            pool = nc.gpsimd

            def select(p):
                kt, q0, _ = KEY_PIECES[p]
                if not DIAGONAL[p]:
                    return
                block = p1[:, P1_AT[kt]:P1_AT[kt] + P]
                pool.wait_ge(p1_exp, NP * n + p + 1).then_inc(p1_seen, 1)
                pool.affine_select(out=block, in_=block, compare_op=ALU.is_ge, fill=0.0, base=0,
                                   pattern=[[1, P]], channel_multiplier=-1).then_inc(p1_sel, 1)

            pool_rstd("att1", n, 0)
            yield
            pool_rstd("att1", n, 1)
            for _ in range(11):
                yield
            for p in range(NP + 2):
                if p >= 2:
                    select(p - 2)
                yield
                if p < NP:
                    w = KEY_PIECES[p][2] - KEY_PIECES[p][1]
                    pool.wait_ge(sq_ready, NP * n + p + 1)
                    pool.tensor_tensor(sq[:, p % 2, 0, 0:w], sq[:, p % 2, 0, 0:w],
                                       sq[:, p % 2, 1, 0:w], ALU.add).then_inc(sum_ready, 1)
                yield
                yield

        def pool_ffn(s, src, n):
            pool = nc.gpsimd

            def difference(h):
                pool.wait_ge(xt_ready[s], 4 * n + 2 * h + 2)
                if h == 1:
                    pool.wait_ge(k_full[s], 4 * n + 2)
                lo = HALF * h
                pool.tensor_tensor(xk[:, :, :], xtb[:, :, 1 + lo:1 + lo + HALF], xtb[:, :, lo:lo + HALF],
                                   ALU.subtract).then_inc(diff_done[s], 1)

            def square_k(h, j):
                pool.wait_ge(kr_ready[s], 4 * n + 2 * h + j + 1)
                pool.tensor_tensor(ka[:, j, :], kr[:, j, :], kr[:, j, :],
                                   ALU.mult).then_inc(ka_ready[s], 1)

            def add(h):
                pool.wait_ge(tm_ready[s], 4 * n + 2 * h + 2)
                x_half = src[:, TPH * h:TPH * (h + 1), :]
                pool.tensor_tensor(x_half, x_half, tm[:, :, :], ALU.add).then_inc(x_added[s], 1)

            pool_rstd(s, n, 0)
            yield
            pool_rstd(s, n, 1)
            yield
            yield
            difference(0)
            yield
            yield
            yield
            square_k(0, 0)
            yield
            square_k(0, 1)
            yield
            difference(1)
            yield
            yield
            yield
            add(0)
            yield
            square_k(1, 0)
            yield
            square_k(1, 1)
            yield
            yield
            yield
            yield
            add(1)

        def pool_proj3(n):
            pool_rstd("proj3", n, 0)
            yield
            pool_rstd("proj3", n, 1)
            yield
            yield
            yield
            yield
            yield
            for j in range(8):
                nc.gpsimd.wait_ge(mid_done, 8 * n + j + 1)
                nc.gpsimd.tensor_tensor(parts[:, j % 2, LO, :], x32[:, j % 2, :], parts[:, j % 2, MID, :],
                                        ALU.subtract).then_inc(lo_done, 1)
                yield
            yield

        def sp_att1(n):
            if isinstance(n, int) and n < 2:
                for h in range(2):
                    sp_load(n, h)
            for _ in range(N_ATT1):
                yield

        def sp_proj3(n):
            for _ in range(6):
                yield
            for j in range(8):
                h, kq, ht = j // 4, (j // NHT) % 2, j % NHT
                nc.sync.wait_ge(lo_done, 8 * n + j + 1)
                nc.sync.dma_start(
                    parts_dram[n, kq, ht].rearrange("r d h n -> (d h) r n")[:, :, HALF * h:HALF * (h + 1)],
                    parts[:, j % 2, :, :]).then_inc(part_stored[j % 2], 16)
                yield
            for g in (1, 2):
                sp_stack(n, g)
            yield

        def sp_load(n, h):
            if not (isinstance(n, int) and n == 0):
                nc.sync.wait_ge(xb_copied[h], 16 * n)
                nc.sync.wait_ge(xh_ready["proj3"], 2 * n)
            nc.sync.dma_start(xa[:, TPH * h:TPH * (h + 1), :],
                              x_tok[n][:, TPH * h:TPH * (h + 1), :]).then_inc(x_loaded[h], 16)

        def sp_copy(n, h):
            nc.sync.wait_ge(x_added["ffn2"], 2 * n + h + 1)
            if not (isinstance(n, int) and n == 0):
                nc.sync.wait_ge(out_stored[h], 16 * n)
            nc.sync.dma_start(xb[:, TPH * h:TPH * (h + 1), :], xa[:, TPH * h:TPH * (h + 1), :]
                              ).then_inc(xb_copied[h], 16)

        def sp_store(n, h):
            nc.sync.wait_ge(x_added["ffn4"], 2 * n + h + 1)
            nc.sync.dma_start(out_tok[n][:, TPH * h:TPH * (h + 1), :], xb[:, TPH * h:TPH * (h + 1), :]
                              ).then_inc(out_stored[h], 16)

        def sp_stack(n, g):
            r = STACK_OF[g]
            ht, h0 = g // 2, GH * (g % 2)
            if g == 3:
                nc.sync.wait_ge(s_full, GH * NP * (NG * n + 1))
            elif not (isinstance(n, int) and n == 0):
                nc.sync.wait_ge(s_full, GH * NP * (NG * (n - 1) + (NG if g == 0 else g + 1)))
            for k in range(2):
                nc.sync.wait_ge(part_stored[k], 64 * n + 64)
            src = parts_dram[n]

            def copy(to, kq, slot, part, count):
                nc.sync.dma_start(
                    to[HD * slot:HD * (slot + count), :, :],
                    src[kq, ht, part:part + count].rearrange("r d h n -> (r d) h n")[:, h0:h0 + GH, :]
                ).then_inc(stack_ready[r], 16)

            copy(ks[r], 0, 0, HI, 3)
            copy(ks[r], 0, 3, HI, 2)
            copy(ks[r], 0, 5, HI, 1)
            for slot, part in enumerate(Q_SLOTS):
                copy(qs[r], 1, slot, part, 1)

        emptied = [None, None]

        def side_job(k, taken, value):
            if emptied[k] is not None:
                nc.tensor.wait_ge(*emptied[k])
            emptied[k] = (taken, value)
            return side[k]

        def pe_transposed(s, src, n, h):
            nc.tensor.wait_ge(xh_ready[s], 2 * n + h + 1)
            for c in range(NC):
                bank = side_job(c, xt_ready[s], 4 * n + 2 * h + c + 1)
                for t in range(TPH):
                    mm = nc.tensor.transpose(bank[:, P * t:P * (t + 1)], src[:, t, P * c:P * (c + 1)],
                                             ident[:, :])
                mm.then_inc(tr_full[s], 1)

        def pe_att1(n):
            pe = nc.tensor

            def values(t):
                if t % TPH == 0:
                    pe.wait_ge(xt_ready["att1"], 4 * n + 2 * (t // TPH) + 2)
                bank = side_job(t % 2, vp_ready, 8 * n + t + 1)
                for c in range(NC):
                    mm = pe.matmul(bank[:, 0:C + 3], xta[:, c, P * t:P * (t + 1)], wvp[:, c, :],
                                   start=(c == 0), stop=(c == NC - 1))
                mm.then_inc(v1_full, 1)

            def positions(c, h):
                pe.wait_ge(vp_ready, 8 * n + TPH * (h + 1))
                bank = side_job((3 * h + c) % 2, pb_ready, 6 * n + 3 * h + c + 1)
                for t in range(TPH):
                    mm = pe.transpose(bank[:, P * t:P * (t + 1)],
                                      vp[:, TPH * h + t, POS + c:POS + c + 1].to_broadcast([P, P]),
                                      ident[:, :])
                mm.then_inc(pb_full, 1)

            def attend(t):
                m = t + 1 if t < TPH else TPH + t + 1
                pe.wait_ge(p1_exp, NP * n + m)
                pe.wait_ge(p1_sel, NT * n + t + 1)
                bank = side_job(t % 2, x1_done, 8 * n + t + 1)
                for kt in range(t + 1):
                    at = P1_AT[kt] + P * (t - kt)
                    mm = pe.matmul(bank[:, 0:VC], p1[:, at:at + P], vp[:, kt, :],
                                   start=(kt == 0), stop=(kt == t))
                mm.then_inc(pv1_full, 1)

            yield
            yield
            pe_transposed("att1", xha, n, 0)
            yield
            yield
            pe_transposed("att1", xha, n, 1)
            yield
            for t in range(0, NT, 2):
                values(t)
                values(t + 1)
                yield
            for c, h in ((0, 0), (2, 0), (1, 1)):
                positions(c, h)
                positions((c + 1) % 3, h if c < 2 else 1)
                yield
            for p in range(NP + 2):
                yield
                for t in summed_after(p):
                    attend(t)
                yield
                yield

        def pe_ffn(s, n):
            pe = nc.tensor

            def keys(h, j):
                pe.wait_ge(xk_ready[s], 2 * n + h + 1)
                bank = side_job(j, kr_ready[s], 4 * n + 2 * h + j + 1)
                for c in range(NC):
                    mm = pe.matmul(bank[:, :], wkT[:, c, P * j:P * (j + 1)], xk[:, c, :],
                                   start=(c == 0), stop=(c == NC - 1))
                mm.then_inc(k_full[s], 1)

            def pair(h, j, lhs, rhs, full, taken):
                bank = side_job(j, taken, 4 * n + 2 * h + j + 1)
                for t in range(2):
                    at = P * (2 * j + t)
                    for c in range(NC):
                        mm = pe.matmul(bank[:, C * t:C * (t + 1)], lhs[:, c, at:at + P], rhs[:, c, :],
                                       start=(c == 0), stop=(c == NC - 1))
                mm.then_inc(full, 1)

            def receptance(h, j):
                pe.wait_ge(xr_ready[s], 2 * n + h + 1)
                pair(h, j, xr, wrT, r_full[s], rexp_done[s])

            def values(h, j):
                pe.wait_ge(ka_ready[s], 4 * n + 2 * h + 2)
                pair(h, j, ka, wvT, v_full[s], tm_ready[s])

            yield
            yield
            pe_transposed(s, xhb, n, 0)
            yield
            yield
            pe_transposed(s, xhb, n, 1)
            yield
            for h in range(2):
                for product in (keys, receptance, values):
                    for j in range(2):
                        product(h, j)
                        yield

        def pe_proj3(n):
            pe = nc.tensor
            yield
            yield
            pe_transposed("proj3", xha, n, 0)
            yield
            yield
            pe_transposed("proj3", xha, n, 1)
            yield
            for j in range(8):
                h, kq, ht = j // 4, (j // NHT) % 2, j % NHT
                pe.wait_ge(xt_ready["proj3"], 4 * n + 2 * h + 2)
                bank = side_job(j % 2, x32_ready, 8 * n + j + 1)
                for c in range(NC):
                    mm = pe.matmul(bank[:, :], wkq[:, c, kq, ht, :, :], xta[:, c, HALF * h:HALF * (h + 1)],
                                   start=(c == 0), stop=(c == NC - 1))
                mm.then_inc(kq_full, 1)
                yield
            yield
            yield

        def pe_values3(n):
            for j in range(4):
                bank = side_job(j % 2, v3_ready, 4 * n + j + 1)
                for t in range(2):
                    at = P * (2 * j + t)
                    for c in range(NC):
                        mm = nc.tensor.matmul(bank[:, C * t:C * (t + 1)], xta[:, c, at:at + P],
                                              wv3[:, c, :, :], start=(c == 0), stop=(c == NC - 1))
                mm.then_inc(v3_full, 1)
            yield

        def pe_att3(i, t, s):
            pe = nc.tensor
            heads = range(2 * s, 2 * s + 2)
            e = t - LEAD
            if t < NG * NP and s == 0 and t % NP == 0:
                g = t // NP
                r = STACK_OF[g]
                pe.wait_ge(stack_ready[r], 16 * N_STACK_DMA * (STACK_LOADS[r] * i + STACK_NTH[g] + 1))
            if 0 <= e < NG * NP and s == 0 and e % NP == 0:
                pe.wait_ge(crow_ready, 32 * (NG * i + e // NP + 1))
            for j in heads:
                if t < NG * NP:
                    g, m = divmod(t, NP)
                    tile, k0, k1 = QUERY_PIECES[m]
                    r = STACK_OF[g]
                    k = GH * t + j
                    pe.wait_ge(max_free, GH * NG * NP * i + max(0, k - 1))
                    pe.matmul(max_bank[k % 2][:, 0:k1 - k0], qs[r][0:KROWS, j, P * tile:P * (tile + 1)],
                              ks[r][0:KROWS, j, k0:k1], start=True, stop=True).then_inc(max_full, 1)
                if 0 <= e < NG * NP:
                    g, m = divmod(e, NP)
                    kt, q0, q1 = KEY_PIECES[m]
                    r = STACK_OF[g]
                    k = GH * e + j
                    pe.wait_ge(exp_done, GH * NG * NP * i + max(0, k - 1))
                    pe.matmul(exp_bank[k % 2][:, 0:q1 - q0], ks[r][:, j, P * kt:P * (kt + 1)],
                              qs[r][:, j, q0:q1], start=True, stop=True).then_inc(s_full, 1)
            if s == 0 and 1 <= e <= NG * NP:
                g, m = divmod(e - 1, NP)
                kt, q0, q1 = KEY_PIECES[m]
                h = 0 if m < TPH else 1
                pe.wait_ge(exp_done, GH * (NG * NP * i + e))
                if DIAGONAL[m]:
                    pe.wait_ge(sel_done, NG * NT * i + NT * g + NTH_DIAGONAL[m] + 1)
                if kt == 0:
                    pe.wait_ge(ot_ready, 8 * i + max(0, 2 * g + h - 1))
                for j in range(GH):
                    mm = pe.matmul(o_bank[h][32 * j:32 * j + VW, q0 - HALF * h:q1 - HALF * h],
                                   v3[:, kt, GH * g + j, :], pt[:, (e - 1) % 2, j, 0:q1 - q0],
                                   start=(kt == 0), stop=(q1 - q0 == P), skip_group_check=True)
                mm.then_inc(pv_done, 1)

        def pe_rows3(i, t, s):
            pe = nc.tensor
            e = t - LEAD
            if s == 1:
                return
            if t >= NP + 1 and (t - NP - 1) % NP == 0 and (t - NP - 1) // NP < NG:
                g = (t - NP - 1) // NP
                pe.wait_ge(negmax_ready, NG * i + g + 1)
                bank = side_job(g % 2, negmaxT_ready, NG * i + g + 1)[:, :].bitcast(BF16)
                for c in range(2):
                    mm = pe.transpose(bank[0:GH * NT, P * c:P * (c + 1)],
                                      neg_max[:, c, :, :].rearrange("p j t -> p (j t)"), identb[:, :])
                mm.then_inc(negmaxT_full, 1)
            for h, at in ((0, 7), (1, NP + 3)):
                if e >= at and (e - at) % NP == 0 and (e - at) // NP < NG:
                    g = (e - at) // NP
                    pe.wait_ge(ot_ready, 8 * i + 2 * g + h + 1)
                    bank = side_job(h, on_ready, 8 * i + 2 * g + h + 1)
                    for q in range(TPH):
                        mm = pe.transpose(bank[:, P * q:P * (q + 1)], ot[:, h, P * q:P * (q + 1)], ident[:, :])
                    mm.then_inc(on_full, 1)

        def act_att3(i, t, s):
            act = nc.scalar
            e = t - LEAD
            if 0 <= e < NG * NP:
                m = e % NP
                kt, q0, q1 = KEY_PIECES[m]
                if s == 0:
                    act.wait_ge(pv_done, NG * NP * i + max(0, e - 1))
                for j in range(2 * s, 2 * s + 2):
                    k = GH * e + j
                    act.wait_ge(s_full, GH * NG * NP * i + k + 1)
                    act.activation(pt[:, e % 2, j, 0:q1 - q0], exp_bank[k % 2][:, 0:q1 - q0], ACT.Exp,
                                   scale=SCALE).then_inc(exp_done, 1)
            if s == 0:
                return
            for h, at in ((0, 5), (1, NP + 1)):
                if e >= at and (e - at) % NP == 0 and (e - at) // NP < NG:
                    g = (e - at) // NP
                    act.wait_ge(pv_done, NG * NP * i + NP * g + (TPH if h == 0 else NP))
                    act.wait_ge(on_full, 8 * i + max(0, 2 * g + h - 1))
                    act.activation(ot[:, h, :], o_bank[h][:, :], ACT.Copy).then_inc(ot_ready, 1)

        def dve_att3(i, t, s):
            dve = nc.vector
            if t < NG * NP:
                g, m = divmod(t, NP)
                tile, k0, k1 = QUERY_PIECES[m]
                w = k1 - k0
                if m == 0 and s == 0:
                    dve.wait_ge(negmax_ready, NG * i + g)
                for j in range(2 * s, 2 * s + 2):
                    k = GH * t + j
                    dve.wait_ge(max_full, GH * NG * NP * i + k + 1).then_inc(scores_seen, 1)
                    if k1 == P * (tile + 1):
                        dve.tensor_tensor_reduce(max_bank[k % 2][:, 0:w], max_bank[k % 2][:, 0:w],
                                                 mask[:, HALF - w:HALF], 1.0, LOWEST, ALU.add, ALU.max,
                                                 piece_max[:, j, m:m + 1]).then_inc(max_free, 1)
                    else:
                        dve.tensor_reduce(piece_max[:, j, m:m + 1], max_bank[k % 2][:, 0:w], AX.X,
                                          ALU.max).then_inc(max_free, 1)
                if m == NP - 1 and s == 1:
                    base = 2 * (NG * i + g)
                    dve.wait_ge(max_free, GH * (NG * NP * i + t + 1))
                    dve.tensor_tensor(piece_max[:, :, TPH:NT], piece_max[:, :, TPH:NT],
                                      piece_max[:, :, NT:NP], ALU.max).then_inc(c_step, 1)
                    dve.wait_ge(c_step, base + 1)
                    dve.tensor_scalar(neg_max[:, 0, :, :], piece_max[:, :, 0:NT], -1.0, None,
                                      ALU.mult).then_inc(c_step, 1)
                    dve.wait_ge(c_step, base + 2)
                    dve.scalar_tensor_tensor(out=neg_max[:, 1, :, :], in0=piece_max[:, :, 0:NT],
                                             scalar=-1.0, in1=neg_max[:, 0, :, :], op0=ALU.mult,
                                             op1=ALU.subtract).then_inc(negmax_ready, 1)

        def dve_rows3(i, t, s):
            dve = nc.vector
            if s == 1:
                return
            if t >= NP + 1 and (t - NP - 1) % NP == 0 and (t - NP - 1) // NP < NG:
                g = (t - NP - 1) // NP
                dve.wait_ge(negmaxT_full, NG * i + g + 1)
                dve.wait_ge(crow_ready, 32 * (NG * i + g))
                bank = side[g % 2][:, :].bitcast(BF16)
                dve.tensor_copy(neg_maxT[:, :, :],
                                bank[0:GH * NT, 0:2 * P].rearrange("p (c n) -> p c n", c=2)
                                ).then_inc(negmaxT_ready, 1)
            e = t - LEAD
            for h, at in ((0, 7), (1, NP + 3)):
                if e >= at and (e - at) % NP == 0 and (e - at) // NP < NG:
                    g = (e - at) // NP
                    n = 8 * i + 2 * g + h
                    dve.wait_ge(on_full, n + 1)
                    o = side[h][:, :].rearrange("p (t j d) -> p t j d", t=TPH, j=GH)
                    dve.wait_ge(on_ready, n)
                    dve.reciprocal(rsum[:, :, :], o[:, :, :, HD]).then_inc(rsum_done, 1)
                    dve.wait_ge(rsum_done, n + 1)
                    dve.wait_ge(xb_added, n)
                    dve.tensor_tensor(on[:, :, :, :], o[:, :, :, 0:HD],
                                      rsum[:, :, :].unsqueeze(3).to_broadcast([P, TPH, GH, HD]),
                                      ALU.mult).then_inc(on_ready, 1)

        def pool_att3(i, t, s):
            pool = nc.gpsimd
            e = t - LEAD
            if s == 1 and 0 <= e < NG * NP and DIAGONAL[e % NP]:
                block = pt[:, e % 2, :, 0:P]
                pool.wait_ge(exp_done, GH * (NG * NP * i + e + 1)).then_inc(exp_seen, 1)
                pool.affine_select(out=block, in_=block, compare_op=ALU.is_ge, fill=0.0, base=0,
                                   pattern=[[0, GH], [1, P]], channel_multiplier=-1).then_inc(sel_done, 1)

        def pool_rows3(i, t, s):
            pool = nc.gpsimd
            e = t - LEAD
            if s == 1:
                return
            for h, at in ((0, 7), (1, NP + 3)):
                if e >= at and (e - at) % NP == 0 and (e - at) // NP < NG:
                    g = (e - at) // NP
                    pool.wait_ge(on_ready, 8 * i + 2 * g + h + 1)
                    pool.wait_ge(xb_copied[h], 16 * i + 16)
                    x_half = xb[:, TPH * h:TPH * (h + 1), GH * HD * g:GH * HD * (g + 1)]
                    pool.tensor_tensor(x_half, x_half, on[:, :, :, :].rearrange("p t j d -> p t (j d)"),
                                       ALU.add).then_inc(xb_added, 1)

        def sp_rows3(i, t, s):
            if s == 1:
                return
            if t >= NP + 1 and (t - NP - 1) % NP == 0 and (t - NP - 1) // NP < NG:
                g = (t - NP - 1) // NP
                r = STACK_OF[g]
                nc.sync.wait_ge(negmaxT_ready, NG * i + g + 1)
                for c in range(2):
                    nc.sync.dma_start(qs[r][KROWS + c:KROWS + c + 1, :, :], neg_maxT[:, c, :]
                                      ).then_inc(crow_ready, 16)
            if t == LEAD + NP:
                sp_stack(i, 3)

        def chain(*stages):
            for stage in stages:
                yield from stage

        def run(chunks):
            for _ in chunks:
                pass

        def has_rows(u):
            t, s = divmod(u, 2)
            return s == 0 and any(x >= at and (x - at) % NP == 0 and (x - at) // NP < NG
                                  for x, at in ((t, NP + 1), (t - LEAD, 7), (t - LEAD, NP + 3)))

        def places(count):
            free = [u for u in range(LAST_SIDE) if not has_rows(u)]
            dense = [u for u in free if u < DENSE][:count]
            rest, sparse = free[len(dense):], count - len(dense)
            return dense + [rest[len(rest) * k // sparse] for k in range(sparse)]

        def attend_with(att, rows, i, chunks, count, is_pe):
            at = places(count)
            for u in range(2 * SLOTS):
                t, s = divmod(u, 2)
                att(i, t, s)
                if not is_pe and u - 1 in at:
                    next(chunks)
                rows(i, t, s)
                if is_pe and u in at:
                    next(chunks)

        N_ATT1, N_FFN, N_PROJ3 = 12 + 3 * (NP + 2), 17, 15
        N_BEFORE = N_ATT1 + N_FFN + N_PROJ3
        N_LAST = 2

        def schedule(eng, att, rows, before, first, ffn4, last, enter=None):
            def attend(i, chunks, count):
                attend_with(att, rows, i, chunks, count, enter is not None)

            run(before(0))
            run(first(0))
            attend(0, before(1), N_BEFORE)
            run(first(1))
            with eng.Fori(0, B - 2) as r:
                if enter:
                    enter(r + 1)
                attend(r + 1, chain(ffn4(r), last(r), before(r + 2)), N_FFN + N_LAST + N_BEFORE)
                run(first(r + 2))
            if enter:
                enter(B - 1)
            attend(B - 1, chain(ffn4(B - 2), last(B - 2)), N_FFN + N_LAST)
            run(ffn4(B - 1))
            run(last(B - 1))

        def nothing(n):
            yield

        def idle(n):
            for _ in range(N_LAST):
                yield

        def no_ffn(n):
            for _ in range(N_FFN):
                yield

        block = ctx.enter_context(nc.Block())

        @block.sync
        def _(sp):
            for k, w in enumerate((wv, wo, w_r, w_k, w_v)):
                sp.dma_start(raw[:, k, :, :], w.rearrange("(a p) c -> p a c", p=P)).then_inc(raw_loaded, 16)
            sp.dma_start(raw3d, w3d).then_inc(raw_loaded, 16)
            for a in range(NC):
                sp.dma_start(raw_kqv[:, a, :, :],
                             wkqv[:, P * a:P * (a + 1), :].rearrange("h c f -> c h f")).then_inc(raw_loaded, 16)
            for row, v in ((bv_row, bv), (mur_row, mu_r), (muk_row, mu_k)):
                sp.dma_start(row, v.rearrange("(a n) -> a n", a=1)).then_inc(rows_loaded, 16)
            sp.dma_start(rows[:, 3 * C:3 * C + H * 48],
                         bkqv.rearrange("(a h) f -> a (h f)", a=1)).then_inc(rows_loaded, 16)
            sp.dma_start(bo_all, bo.rearrange("(a n) -> a n", a=1).to_broadcast([P, C])).then_inc(rows_loaded, 16)
            sp.dma_start(bias_vp[:, C:C + 3],
                         b3d.rearrange("(a n) -> a n", a=1).to_broadcast([P, 3])).then_inc(rows_loaded, 16)
            sp.dma_start(bv3[:, :, :], bkqv[:, 2 * HD:3 * HD].unsqueeze(0).to_broadcast([P, H, HD])
                         ).then_inc(rows_loaded, 16)

            def before(n):
                return chain(sp_att1(n), no_ffn(n), sp_proj3(n))

            def first(n):
                if isinstance(n, int) and n == 0:
                    for h in range(2):
                        sp_copy(0, h)
                sp_stack(n, 0)
                yield

            def last(n):
                for h in range(2):
                    sp_store(n, h)
                    if not (isinstance(n, int) and n == B - 1):
                        sp_copy(n + 1, h)
                    if not isinstance(n, int):
                        sp_load(n + 2, h)
                for _ in range(N_LAST):
                    yield

            schedule(sp, lambda i, t, s: None, sp_rows3, before, first, no_ffn, last)
            for h in range(2):
                sp.wait_ge(out_stored[h], 16 * B)

        @block.gpsimd
        def _(pool):
            pool.memset(ident[:, :], 0.0).then_inc(cleared, 1)
            pool.memset(identb[:, :], 0.0).then_inc(cleared, 1)
            pool.memset(mask[:, :], 0.0).then_inc(cleared, 1)
            pool.wait_ge(cleared, 3)
            for m in (ident, identb):
                pool.affine_select(out=m[:, :], in_=m[:, :], compare_op=ALU.not_equal, fill=1.0, base=0,
                                   pattern=[[-1, P]], channel_multiplier=1).then_inc(consts_ready, 1)
            tail = mask[:, HALF - P:HALF]
            pool.affine_select(out=tail, in_=tail, compare_op=ALU.is_ge, fill=LOWEST, base=0,
                               pattern=[[-1, P]], channel_multiplier=1).then_inc(consts_ready, 1)
            pool.memset(minus_half[:, :], -0.5).then_inc(consts_ready, 1)
            pool.memset(xtb[:, :, 0:1], 0.0).then_inc(consts_ready, 1)
            pool.memset(vp[:, :, ONE:ONE + 1], 1.0).then_inc(consts_ready, 1)
            pool.memset(v3[:, :, :, HD:VW], 1.0).then_inc(consts_ready, 1)
            pool.wait_ge(consts_ready, 7)
            for r in range(STACKS):
                pool.memset(ks[r][KROWS:SROWS, :, :], 1.0).then_inc(consts_ready, 1)

            def before(n):
                return chain(pool_att1(n), pool_ffn("ffn2", xa, n), pool_proj3(n))

            pool.wait_ge(consts_ready, 7 + STACKS)
            pool.wait_ge(weights_ready, 1)
            schedule(pool, pool_att3, pool_rows3, before, nothing, lambda n: pool_ffn("ffn4", xb, n), idle)

        @block.scalar
        def _(act):
            def before(n):
                return chain(act_att1(n), act_ffn("ffn2", n), act_proj3(n))

            act.preload_act_table_set("natural_log_exp_and_others")
            act.wait_ge(weights_ready, 1)
            schedule(act, act_att3, lambda i, t, s: None, before, nothing,
                     lambda n: act_ffn("ffn4", n), idle)

        @block.vector
        def _(dve):
            for k in range(2):
                dve.memset(o_bank[k][:, :], 0.0)
            dve.wait_ge(raw_loaded, 16 * 8)
            dve.wait_ge(rows_loaded, 16 * 7)
            for q in range(2):
                dve.tensor_copy(bkq_row[:, q, :, :, :],
                                kqv_row[:, :, :, HD * q:HD * (q + 1)].rearrange("p t h d -> p t d h")
                                ).then_inc(rows_ready, 1)
            kqv = raw_kqv.rearrange("p a (t h) f -> p a t h f", t=NHT)
            for a in range(NC):
                for q in range(2):
                    for t in range(NHT):
                        dve.tensor_copy(wkq[:, a, q, t, :, :],
                                        kqv[:, a, t, :, HD * q:HD * (q + 1)].rearrange("p h d -> p d h"))
            dve.tensor_copy(wv3[:, :, :, :], raw_kqv[:, :, :, 2 * HD:3 * HD])
            job = 0
            for dst in (wvp, wrT, wkT, wvT):
                for a in range(NC):
                    dve.wait_ge(setup_full, job + 1)
                    dve.tensor_copy(dst[:, a, 0:C], side[job % 2][:, 0:C]).then_inc(setup_taken, 1)
                    job += 1
            dve.wait_ge(setup_full, job + 1)
            dve.tensor_copy(cols[:, :], side[job % 2][:, 0:10]).then_inc(setup_taken, 1)
            job += 1
            dve.memset(bv_wide, 1.0).then_inc(bv_spread, 1)
            dve.wait_ge(setup_taken, job)
            dve.wait_ge(bv_spread, 1)
            for a in range(NC):
                dve.tensor_scalar(bv_wide[:, a, :], bv_wide[:, a, :], cols[:, BV + a:BV + a + 1], None,
                                  ALU.mult).then_inc(bv_spread, 1)
            dve.wait_ge(setup_full, job + 1)
            dve.tensor_copy(wvp[:, :, C:C + 3],
                            side[job % 2][:, 0:3 * NC].rearrange("p (a k) -> p a k", a=NC)
                            ).then_inc(setup_taken, 1)
            job += 1
            dve.wait_ge(setup_full, job + 1)
            dve.tensor_tensor(bias_vp[:, 0:C], side[job % 2][:, 0:C], bo_all, ALU.add).then_inc(setup_taken, 1)
            job += 1
            dve.wait_ge(setup_full, job + 2)
            for a in range(NC):
                dve.tensor_copy(wvp[:, a, 0:C], side[job % 2][:, 0:C]).then_inc(setup_taken, 1)
                job += 1
            dve.memset(rinv1[:, :], 0.0).then_inc(weights_ready, 1)
            dve.wait_ge(weights_ready, 1)
            dve.wait_ge(consts_ready, 7 + STACKS)

            def before_ffn2(n):
                if isinstance(n, int) and n < 2:
                    return x_added["ffn2"], 2 * n
                return x_added["ffn4"], 2 * (n - 1)

            def before_ffn4(n):
                if isinstance(n, int) and n == B - 1:
                    return x_added["ffn4"], 2 * n
                return x_added["ffn2"], 2 * (n + 2)

            def before(n):
                return chain(dve_att1(n), dve_ffn("ffn2", xa, n, before_ffn2(n)), dve_proj3(n))

            schedule(dve, dve_att3, dve_rows3, before, dve_values3,
                     lambda n: dve_ffn("ffn4", xb, n, before_ffn4(n)), idle)

        @block.tensor
        def _(pe):
            pe.wait_ge(consts_ready, 7 + STACKS)
            pe.wait_ge(raw_loaded, 16 * 8)
            pe.wait_ge(rows_loaded, 16 * 7)
            pe.wait_ge(rows_ready, 2)
            jobs = [0]

            def setup_job():
                jobs[0] += 1
                return side_job((jobs[0] - 1) % 2, setup_taken, jobs[0])

            for k in (1, 2, 3, 4):
                for c in range(NC):
                    bank = setup_job()
                    for a in range(NC):
                        mm = pe.transpose(bank[:, P * a:P * (a + 1)], raw[:, k, a, P * c:P * (c + 1)], ident[:, :])
                    mm.then_inc(setup_full, 1)
            bank = setup_job()
            pieces = [row[:, P * a:P * (a + 1)] for row in (bv_row, mur_row, muk_row) for a in range(NC)]
            pieces += [bkq_row[:, q, t, :, :] for q in range(2) for t in range(NHT)]
            for k, piece in enumerate(pieces):
                mm = pe.matmul(bank[:, k:k + 1], piece, ident[0:1, 0:1], start=True, stop=True)
            mm.then_inc(setup_full, 1)
            bank = setup_job()
            for a in range(NC):
                mm = pe.transpose(bank[:, 3 * a:3 * (a + 1)], raw3d[:, P * a:P * (a + 1)], ident[0:3, 0:3])
            mm.then_inc(setup_full, 1)
            pe.wait_ge(bv_spread, 3)
            bank = setup_job()
            for a in range(NC):
                mm = pe.matmul(bank[:, 0:C], bv_wide[:, a, :], wvp[:, a, 0:C], start=(a == 0), stop=(a == NC - 1))
            mm.then_inc(setup_full, 1)
            for c in range(NC):
                bank = setup_job()
                for a in range(NC):
                    mm = pe.matmul(bank[:, 0:C], raw[:, 0, a, P * c:P * (c + 1)], wvp[:, a, 0:C],
                                   start=(a == 0), stop=(a == NC - 1))
                mm.then_inc(setup_full, 1)
            pe.wait_ge(weights_ready, 1)

            def enter(n):
                for k in range(2):
                    emptied[k] = (v3_ready, 4 * n + 3 + k)

            def before(n):
                return chain(pe_att1(n), pe_ffn("ffn2", n), pe_proj3(n))

            schedule(pe, pe_att3, pe_rows3, before, pe_values3, lambda n: pe_ffn("ffn4", n), idle, enter)


_INS = ['L0_attn_a_x', 'L0_attn_a_wq', 'L0_attn_a_bq', 'L0_attn_a_wk', 'L0_attn_a_bk', 'L0_attn_a_wv',
        'L0_attn_a_bv', 'L0_attn_a_wo', 'L0_attn_a_bo', 'L0_attn_a_w3d', 'L0_attn_a_b3d',
        'L0_attn_b_Wkqv', 'L0_attn_b_bkqv', 'L0_ffn_W_r', 'L0_ffn_W_k', 'L0_ffn_W_v', 'L0_ffn_mu_r',
        'L0_ffn_mu_k']
_OUTS = [((B, S, C), 'float32')]


def kernel(**inputs):
    import numpy as _np
    import concourse.bacc as _bacc
    from concourse import mybir as _mybir
    from concourse.bass_utils import run_bass_kernel_spmd as _run

    nc = _bacc.Bacc("TRN2", target_bir_lowering=False, num_devices=1)
    arrays, args = {}, []
    for name in _INS:
        a = _np.ascontiguousarray(inputs[name])
        arrays[f"in_{name}_dram"] = a
        args.append(nc.dram_tensor(f"in_{name}_dram", a.shape, _mybir.dt.from_np(a.dtype), kind="ExternalInput").ap())
    for i, (shape, dtype) in enumerate(_OUTS):
        dt = _mybir.dt.from_np(_np.dtype(dtype))
        args.append(nc.dram_tensor(f"out_{i}_dram", shape, dt, kind="ExternalOutput").ap())
    bass_hybrid(nc, *args)
    r = _run(nc, [arrays], core_ids=[0])
    return r.results[0]["out_0_dram"]
```

```python
from contextlib import ExitStack

import concourse.bass as bass
from concourse import mybir

F32 = mybir.dt.float32
BF16 = mybir.dt.bfloat16
ALU = mybir.AluOpType
ACT = mybir.ActivationFunctionType
AX = mybir.AxisListType

P = 128
B, S, C = 8, 1024, 256
H, HD = 16, 16
NT = S // P
NC = C // P
HALF = S // 2
TPH = HALF // P
GH = 4
NG = H // GH
H8 = P // HD
NHT = H // H8
EPS = 1e-5
SCALE = HD ** -0.5
TINY = 1e-18
LOWEST = -3.0e38
VC = C + 4
POS, ONE = C, C + 3
VW = HD + 1

HI, MID, LO = 0, 1, 2
K_SLOTS = (HI, MID, LO, HI, MID, HI)
Q_SLOTS = (HI, HI, HI, MID, MID, LO)
KROWS = HD * len(K_SLOTS)
SROWS = KROWS + 2
MAX_BANKS, EXP_BANKS = 3, 2
STACKS = 3
STACK_OF = (0, 1, 2, 0)
STACK_LOADS = (2, 1, 1)
STACK_NTH = (0, 0, 0, 1)
N_STACK_DMA = 9

KEY_PIECES = [(kt, P * kt, HALF) for kt in range(TPH)] + \
             [(kt, max(HALF, P * kt), S) for kt in range(NT)]
DIAGONAL = [q0 == P * kt for kt, q0, _ in KEY_PIECES]
NTH_DIAGONAL = [sum(DIAGONAL[:m]) for m in range(len(KEY_PIECES))]
QUERY_PIECES = [(i, 0, P * (i + 1)) for i in range(TPH)] + \
               [(i, 0, HALF) for i in range(TPH, NT)] + \
               [(i, HALF, P * (i + 1)) for i in range(TPH, NT)]
NP = len(KEY_PIECES)
assert NP == len(QUERY_PIECES) == 12
LEAD = NP + 2
SLOTS = NG * NP + LEAD + 3
DENSE = 2 * LEAD
BACK = 2 * (LEAD + (NG - 1) * NP + TPH + 2) + 1
P1_AT = [sum(S - P * j for j in range(kt)) for kt in range(NT)]
P1_COLS = sum(S - P * j for j in range(NT))


def bass_hybrid(nc, x, wq, bq, wk, bk, wv, bv, wo, bo, w3d, b3d, wkqv, bkqv, w_r, w_k, w_v,
                mu_r, mu_k, out):
    parts_dram = nc.dram_tensor("parts_dram", [B, 2, NHT, 3, HD, H8, S], BF16, kind="Internal").ap()

    nc.disable_value_cache = True

    with ExitStack() as ctx:
        def sb(name, shape, dt=F32):
            return ctx.enter_context(nc.sbuf_tensor(name, shape, dt))

        def psum(name):
            return ctx.enter_context(nc.psum_tensor(name, [P, HALF], F32))

        def sem(name):
            return ctx.enter_context(nc.semaphore(name))

        side = [psum(f"side{k}") for k in range(2)]
        max_bank = [psum(f"max_bank{k}") for k in range(MAX_BANKS)]
        exp_bank = [psum(f"exp_bank{k}") for k in range(EXP_BANKS)]
        o_bank = psum("o_bank")

        ident = sb("ident", [P, P])
        identb = sb("identb", [P, P], BF16)
        mask = sb("mask", [P, HALF])
        wvp = sb("wvp", [P, NC, C + 3])
        bias_vp = sb("bias_vp", [P, C + 3])
        wrT = sb("wrT", [P, NC, C])
        wkT = sb("wkT", [P, NC, C])
        wvT = sb("wvT", [P, NC, C])
        wkq = sb("wkq", [P, NC, 2, NHT, HD, H8])
        wv3 = sb("wv3", [P, NC, H, HD])
        bv3 = sb("bv3", [P, H, HD])
        cols = sb("cols", [P, 10])
        BV, MUR, MUK, BKQ = 0, 2, 4, 6

        xa = sb("xa", [P, NT, C])
        xb = sb("xb", [P, NT, C])
        xha = sb("xha", [P, TPH, C])
        xhb = sb("xhb", [P, TPH, C])
        xta = sb("xta", [P, NC, S])
        xtb = sb("xtb", [P, NC, 1 + S])
        st = sb("st", [P, TPH, 6])
        mv = sb("mv", [P, TPH, 2])
        var_eps = sb("var_eps", [P, TPH])
        rstd = sb("rstd", [P, TPH])
        minus_half = sb("minus_half", [P, TPH])
        vp = sb("vp", [P, NT, VC])
        neg_pos = sb("neg_pos", [P, NT, 3])
        pb = sb("pb", [P, 3, S])
        sq = sb("sq", [P, 2, 3, HALF])
        p1 = sb("p1", [P, P1_COLS])
        rinv1 = sb("rinv1", [P, NT])
        xr, xk, ka = (pb[:, k, :].rearrange("p (c n) -> p c n", c=NC) for k in range(3))
        kr = sq[:, 0, 0:2, :]
        th = sq[:, 1, 0:2, :].rearrange("p a (b c) -> p (a b) c", c=C)
        tm = sb("tm", [P, TPH, C])
        diff = tm[:, :, :].rearrange("p a b -> p (a b)").rearrange("p (c n) -> p c n", c=NC)
        x32 = sb("x32", [P, 2, HALF])
        parts = sb("parts", [P, 2, 3, HALF], BF16)
        v3 = sb("v3", [P, NT, H, VW])
        ks = [sb(f"ks{r}", [SROWS, GH, S], BF16) for r in range(STACKS)]
        qs = [sb(f"qs{r}", [SROWS, GH, S], BF16) for r in range(STACKS)]
        piece_max = sb("piece_max", [P, GH, NP])
        neg_max = sb("neg_max", [P, 2, GH, NT], BF16)
        neg_maxT = sb("neg_maxT", [GH * NT, 2, P], BF16)
        pt = sb("pt", [P, 2, GH, HALF])
        ot = sb("ot", [P, 2, HALF])
        rsum = sb("rsum", [P, TPH, GH])
        on = sb("on", [P, TPH, GH, HD])

        raw = pt[:, :, :, :].rearrange("p a b n -> p (a b n)")[:, 0:5 * NC * C].rearrange(
            "p (w a n) -> p w a n", w=5, a=NC)
        raw3d = ot[0:3, 0, 0:C]
        raw_kqv = p1[:, 0:NC * H * 48].rearrange("p (a h f) -> p a h f", a=NC, h=H)
        rows = sq[0:1, :, :, :].rearrange("p a b n -> p (a b n)")
        bv_row, mur_row, muk_row = (rows[:, k * C:(k + 1) * C] for k in range(3))
        kqv_row = rows[:, 3 * C:3 * C + H * 48].rearrange("p (t h f) -> p t h f", t=NHT, h=H8)
        bkq_row = rows[:, 3 * C + H * 48:3 * C + H * 48 + 2 * C].rearrange(
            "p (q t d h) -> p q t d h", q=2, t=NHT, d=HD)
        bo_all = tm[:, 0, :]
        bv_wide = tm[:, 1, :].rearrange("p (a n) -> p a n", a=NC)

        raw_loaded, rows_loaded, cleared, consts_ready, rows_ready, bv_spread, weights_ready = (
            sem(n) for n in ("raw_loaded", "rows_loaded", "cleared", "consts_ready", "rows_ready",
                             "bv_spread", "weights_ready"))
        setup_full, setup_taken = sem("setup_full"), sem("setup_taken")
        x_loaded = [sem(f"x_loaded{h}") for h in range(2)]
        xb_copied = [sem(f"xb_copied{h}") for h in range(2)]
        out_stored = [sem(f"out_stored{h}") for h in range(2)]
        STAGES = ("att1", "ffn2", "proj3", "ffn4")
        ln_step = {s: sem(f"{s}_ln_step") for s in STAGES}
        rstd_ready = {s: sem(f"{s}_rstd_ready") for s in STAGES}
        xh_ready = {s: sem(f"{s}_xh_ready") for s in STAGES}
        tr_full = {s: sem(f"{s}_tr_full") for s in STAGES}
        xt_ready = {s: sem(f"{s}_xt_ready") for s in STAGES}
        v1_full, vp_ready, neg_ready, pb_full, pb_ready = (
            sem(n) for n in ("v1_full", "vp_ready", "neg_ready", "pb_full", "pb_ready"))
        sq_ready, sum_ready, dist2_ready, log_done, dist_done, p1_exp, p1_sel, pv1_full, rinv_done, x1_done = (
            sem(n) for n in ("sq_ready", "sum_ready", "dist2_ready", "log_done", "dist_done", "p1_exp", "p1_sel",
                             "pv1_full", "rinv_done", "x1_done"))
        FF = ("ffn2", "ffn4")
        (diff_done, xr_ready, xk_ready, k_full, r_full, kr_ready, ka_ready, rexp_done, rlog_done,
         th_ready, v_full, tm_ready, x_added) = (
            {s: sem(f"{s}_{n}") for s in FF} for n in (
                "diff_done", "xr_ready", "xk_ready", "k_full", "r_full", "kr_ready", "ka_ready",
                "rexp_done", "rlog_done", "th_ready", "v_full", "tm_ready", "x_added"))
        kq_full, x32_ready, hi_done, rest_done, mid_done, lo_done, v3_full, v3_ready = (
            sem(n) for n in ("kq_full", "x32_ready", "hi_done", "rest_done", "mid_done", "lo_done",
                             "v3_full", "v3_ready"))
        part_stored = [sem(f"part_stored{k}") for k in range(2)]
        stack_ready = [sem(f"stack_ready{r}") for r in range(STACKS)]
        max_full, max_free, c_step, negmax_ready, negmaxT_full, negmaxT_ready, crow_ready = (
            sem(n) for n in ("max_full", "max_free", "c_step", "negmax_ready", "negmaxT_full",
                             "negmaxT_ready", "crow_ready"))
        s_full, exp_done, sel_done, pv_done, ot_ready, on_full, rsum_done, on_ready, xb_added = (
            sem(n) for n in ("s_full", "exp_done", "sel_done", "pv_done", "ot_ready",
                             "on_full", "rsum_done", "on_ready", "xb_added"))
        o_full = [sem(f"o_full{h}") for h in range(2)]
        third_ready = sem("third_ready")
        rows_of_ones = sem("rows_of_ones")
        stats_seen, p1_seen, exp_seen, scores_seen = (
            sem(name) for name in ("stats_seen", "p1_seen", "exp_seen", "scores_seen"))

        x_tok = x.rearrange("b (t p) c -> b p t c", p=P)
        out_tok = out.rearrange("b (t p) c -> b p t c", p=P)


        def summed_after(p):
            return [t for t in range(NT) if (t if t < TPH else TPH + t) == p - 2]

        def normaliser(s, src, dst, n, ready):
            dve = nc.vector

            def statistics(h):
                base = 6 * n + 3 * h
                ready(h)
                for t in range(TPH):
                    last = dve.bn_stats(st[:, t, :], src[:, TPH * h + t, :])
                last.then_inc(ln_step[s], 1)
                dve.wait_ge(ln_step[s], base + 1).then_inc(stats_seen, 1)
                for t in range(TPH):
                    last = dve.bn_aggr(mv[:, t, :], st[:, t, :])
                last.then_inc(ln_step[s], 1)
                dve.wait_ge(ln_step[s], base + 2)
                dve.tensor_scalar(var_eps[:, :], mv[:, :, 1], EPS, None, ALU.add).then_inc(ln_step[s], 1)

            def apply(h):
                dve.wait_ge(rstd_ready[s], 2 * n + h + 1)
                if h == 1:
                    dve.wait_ge(tr_full[s], 4 * n + 2)
                for t in range(TPH):
                    last = dve.tensor_scalar(dst[:, t, :], src[:, TPH * h + t, :], mv[:, t, 0:1],
                                             rstd[:, t:t + 1], ALU.subtract, ALU.mult)
                last.then_inc(xh_ready[s], 1)

            return statistics, apply

        def dve_normalise(s, src, dst, n, ready):
            statistics, apply = normaliser(s, src, dst, n, ready)
            statistics(0)
            yield
            apply(0)
            nc.vector.wait_ge(xh_ready[s], 2 * n + 1)
            statistics(1)
            yield
            yield
            apply(1)
            yield

        def dve_att1(n):
            dve = nc.vector

            def loaded(h):
                dve.wait_ge(x_loaded[h], 16 * n + 16)

            def values(t):
                dve.wait_ge(v1_full, 8 * n + t + 1)
                dve.tensor_tensor(vp[:, t, 0:C + 3], side[t % 2][:, 0:C + 3], bias_vp[:, :],
                                  ALU.add).then_inc(vp_ready, 1)

            def negate(h):
                dve.wait_ge(vp_ready, 8 * n + TPH * (h + 1))
                dve.tensor_scalar(neg_pos[:, TPH * h:TPH * (h + 1), :],
                                  vp[:, TPH * h:TPH * (h + 1), POS:POS + 3], -1.0, None,
                                  ALU.mult).then_inc(neg_ready, 1)

            def distance(p):
                kt, q0, q1 = KEY_PIECES[p]
                w = q1 - q0
                dve.wait_ge(sum_ready, NP * n + p + 1)
                dve.wait_ge(third_ready, NP * n + p + 1)
                dve.scalar_tensor_tensor(out=sq[:, p % 2, 0, 0:w], in0=sq[:, p % 2, 0, 0:w],
                                         scalar=TINY, in1=sq[:, p % 2, 2, 0:w],
                                         op0=ALU.max, op1=ALU.add).then_inc(dist2_ready, 1)

            def residual(t):
                dve.wait_ge(pv1_full, 8 * n + t + 1)
                dve.reciprocal(rinv1[:, t:t + 1], side[t % 2][:, ONE:ONE + 1]).then_inc(rinv_done, 1)
                dve.wait_ge(rinv_done, 8 * n + t + 1)
                dve.scalar_tensor_tensor(out=xa[:, t, :], in0=side[t % 2][:, 0:C],
                                         scalar=rinv1[:, t:t + 1], in1=xa[:, t, :],
                                         op0=ALU.mult, op1=ALU.add).then_inc(x1_done, 1)

            yield from dve_normalise("att1", xa, xha, n, loaded)
            yield
            values(0)
            values(1)
            yield
            values(2)
            values(3)
            negate(0)
            yield
            values(4)
            values(5)
            yield
            values(6)
            values(7)
            negate(1)
            yield
            yield
            yield
            yield
            for p in range(NP + 2):
                yield
                for t in summed_after(p):
                    residual(t)
                yield
                if p < NP:
                    distance(p)
                yield

        def dve_ffn(s, src, n, half=None):
            dve = nc.vector

            def ready(h):
                if s == "ffn2":
                    dve.wait_ge(x1_done, 8 * n + TPH * (h + 1))
                else:
                    dve.wait_ge(xb_added, 8 * n + 2 * (NG - 1) + h + 1)

            def mix(h):
                before = xtb[:, :, HALF * h:HALF * h + HALF]
                for dst, mu, done in ((xk, MUK, xk_ready), (xr, MUR, xr_ready)):
                    if h == 1:
                        dve.wait_ge((k_full if dst is xk else r_full)[s], 4 * n + 2)
                    for c in range(NC):
                        if dst is xk:
                            dve.wait_ge(diff_done[s], 4 * n + 2 * h + c + 1)
                        last = dve.scalar_tensor_tensor(
                            out=dst[:, c, :], in0=diff[:, c, :], scalar=cols[:, mu + c:mu + c + 1],
                            in1=before[:, c, :], op0=ALU.mult, op1=ALU.add)
                    last.then_inc(done[s], 1)

            def gate(h, j):
                if j == 0:
                    dve.wait_ge(xr_ready[s], 2 * n + (h + 1 if half is not None else 2))
                    if h == 1:
                        dve.wait_ge(x_added[s], 2 * n + 1)
                dve.wait_ge(th_ready[s], 4 * n + 2 * h + j + 1)
                dve.wait_ge(v_full[s], 4 * n + 2 * h + j + 1)
                dve.tensor_tensor(tm[:, 2 * j:2 * j + 2, :], th[:, 2 * j:2 * j + 2, :],
                                  side[j][:, :].rearrange("p (t c) -> p t c", c=C),
                                  ALU.mult).then_inc(tm_ready[s], 1)

            if half is not None:
                statistics, apply = normaliser(s, src, xhb, n, ready)
                statistics(half)
                yield
                apply(half)
                yield
                yield
                mix(half)
                yield
                for _ in range(4):
                    yield
                gate(half, 0)
                yield
                gate(half, 1)
                yield
                yield
                return
            yield from dve_normalise(s, src, xhb, n, ready)
            mix(0)
            yield
            for _ in range(4):
                yield
            mix(1)
            gate(0, 0)
            yield
            gate(0, 1)
            yield
            for _ in range(4):
                yield
            gate(1, 0)
            yield
            gate(1, 1)
            yield

        def dve_proj3(n):
            dve = nc.vector

            def ready(h):
                dve.wait_ge(x_added["ffn2"], 2 * n + h + 1)

            def split(j):
                r = j % 2
                if j >= 2:
                    dve.wait_ge(part_stored[r], 64 * n + 16 * (j // 2))
                else:
                    dve.wait_ge(part_stored[r], 64 * n)
                dve.wait_ge(x32_ready, 8 * n + j + 1)
                dve.tensor_copy(parts[:, r, HI, :], x32[:, r, :]).then_inc(hi_done, 1)
                dve.wait_ge(hi_done, 8 * n + j + 1)
                dve.tensor_tensor(x32[:, r, :], x32[:, r, :], parts[:, r, HI, :],
                                  ALU.subtract).then_inc(rest_done, 1)
                dve.wait_ge(rest_done, 8 * n + j + 1)
                dve.tensor_copy(parts[:, r, MID, :], x32[:, r, :]).then_inc(mid_done, 1)

            yield from dve_normalise("proj3", xa, xha, n, ready)
            yield
            yield
            for j in range(8):
                split(j)
                yield
            yield

        def dve_values3(n):
            for j in range(4):
                nc.vector.wait_ge(v3_full, 4 * n + j + 1)
                for t in range(2):
                    last = nc.vector.tensor_tensor(
                        v3[:, 2 * j + t, :, 0:HD],
                        side[j % 2][:, C * t:C * (t + 1)].rearrange("p (h d) -> p h d", d=HD),
                        bv3[:, :, :], ALU.add)
                last.then_inc(v3_ready, 1)
            yield

        def act_transposed(s, dst, off, n, h):
            for c in range(NC):
                nc.scalar.wait_ge(tr_full[s], 4 * n + 2 * h + c + 1)
                nc.scalar.activation(dst[:, c, off + HALF * h:off + HALF * (h + 1)], side[c][:, :],
                                     ACT.Copy).then_inc(xt_ready[s], 1)

        def act_att1(n):
            act = nc.scalar

            def positions(c, h):
                k = 3 * h + c
                act.wait_ge(pb_full, 6 * n + k + 1)
                act.activation(pb[:, c, HALF * h:HALF * (h + 1)], side[k % 2][:, :],
                               ACT.Copy).then_inc(pb_ready, 1)

            def square(p, c):
                if p >= NP:
                    return
                kt, q0, q1 = KEY_PIECES[p]
                w = q1 - q0
                if c == 0:
                    act.wait_ge(neg_ready, 2 * n + kt // TPH + 1)
                    act.wait_ge(pb_ready, 6 * n + (3 if q1 <= HALF else 6))
                    act.wait_ge(p1_exp, NP * n + max(0, p - 1))
                mm = act.activation(sq[:, p % 2, c, 0:w], pb[:, c, q0:q1], ACT.Square,
                                    bias=neg_pos[:, kt, c:c + 1])
                if c == 1:
                    mm.then_inc(sq_ready, 1)
                if c == 2:
                    mm.then_inc(third_ready, 1)

            def transform(p, k):
                if not 0 <= p < NP:
                    return
                kt, q0, q1 = KEY_PIECES[p]
                w = q1 - q0
                d = sq[:, p % 2, 0, 0:w]
                at = P1_AT[kt] + q0 - P * kt
                if k == 0:
                    act.wait_ge(dist2_ready, NP * n + p + 1)
                    act.activation(d, d, ACT.Ln).then_inc(log_done, 1)
                elif k == 1:
                    act.wait_ge(log_done, NP * n + p + 1)
                    act.activation(d, d, ACT.Exp, scale=0.5).then_inc(dist_done, 1)
                else:
                    if p == 0:
                        act.wait_ge(pv1_full, 8 * n)
                    act.wait_ge(dist_done, NP * n + p + 1)
                    act.activation(p1[:, at:at + w], d, ACT.Exp, scale=-SCALE).then_inc(p1_exp, 1)

            yield
            yield
            act.wait_ge(v3_full, 4 * n)
            act_transposed("att1", xta, 0, n, 0)
            yield
            yield
            act_transposed("att1", xta, 0, n, 1)
            yield
            for _ in range(4):
                yield
            positions(0, 0)
            positions(1, 0)
            yield
            positions(2, 0)
            positions(0, 1)
            yield
            positions(1, 1)
            positions(2, 1)
            yield
            for p in range(NP + 2):
                square(p, 0)
                transform(p - 1, 0)
                square(p, 1)
                yield
                transform(p - 1, 1)
                square(p, 2)
                yield
                transform(p - 1, 2)
                yield

        def act_ffn(s, n, half=None):
            act = nc.scalar

            def relu_k(h, j):
                act.wait_ge(k_full[s], 4 * n + 2 * h + j + 1)
                if h == 1:
                    act.wait_ge(ka_ready[s], 4 * n + j + 1)
                act.activation(kr[:, j, :], side[j][:, :], ACT.Relu).then_inc(kr_ready[s], 1)

            def sigmoid(h, j, k):
                job = 4 * n + 2 * h + j + 1
                r = th[:, 2 * j:2 * j + 2, :]
                if k == 0:
                    if h == 1:
                        act.wait_ge(tm_ready[s], 4 * n + j + 1)
                    act.wait_ge(r_full[s], job)
                    act.activation(r, side[j][:, :].rearrange("p (t c) -> p t c", c=C),
                                   ACT.Exp, scale=-1.0).then_inc(rexp_done[s], 1)
                elif k == 1:
                    act.wait_ge(rexp_done[s], job)
                    act.activation(r, r, ACT.Ln, bias=1.0).then_inc(rlog_done[s], 1)
                else:
                    act.wait_ge(rlog_done[s], job)
                    act.activation(r, r, ACT.Exp, scale=-1.0).then_inc(th_ready[s], 1)

            yield
            yield
            act_transposed(s, xtb, 1, n, half or 0)
            yield
            yield
            if half is None:
                act_transposed(s, xtb, 1, n, 1)
                yield
            for h in (range(2) if half is None else (half,)):
                for j in range(2):
                    relu_k(h, j)
                    yield
                sigmoid(h, 0, 0)
                yield
                sigmoid(h, 1, 0)
                sigmoid(h, 0, 1)
                yield
                sigmoid(h, 0, 2)
                sigmoid(h, 1, 1)
                yield
                sigmoid(h, 1, 2)
                yield
            if half is not None:
                yield

        def act_proj3(n):
            act = nc.scalar
            yield
            yield
            act_transposed("proj3", xta, 0, n, 0)
            yield
            yield
            act_transposed("proj3", xta, 0, n, 1)
            yield
            for j in range(8):
                kq, ht = (j // NHT) % 2, j % NHT
                act.wait_ge(kq_full, 8 * n + j + 1)
                if j >= 2:
                    act.wait_ge(lo_done, 8 * n + j - 1)
                else:
                    act.wait_ge(lo_done, 8 * n)
                act.activation(x32[:, j % 2, :], side[j % 2][:, :], ACT.Identity,
                               bias=cols[:, BKQ + 2 * kq + ht:BKQ + 2 * kq + ht + 1]).then_inc(x32_ready, 1)
                yield
            yield
            yield

        def pool_rstd(s, n, h):
            nc.gpsimd.wait_ge(ln_step[s], 6 * n + 3 * h + 3)
            nc.gpsimd.tensor_tensor(rstd[:, :], var_eps[:, :], minus_half[:, :],
                                    ALU.pow).then_inc(rstd_ready[s], 1)

        def pool_att1(n):
            pool = nc.gpsimd

            def select(p):
                kt, q0, _ = KEY_PIECES[p]
                if not DIAGONAL[p]:
                    return
                block = p1[:, P1_AT[kt]:P1_AT[kt] + P]
                pool.wait_ge(p1_exp, NP * n + p + 1).then_inc(p1_seen, 1)
                pool.affine_select(out=block, in_=block, compare_op=ALU.is_ge, fill=0.0, base=0,
                                   pattern=[[1, P]], channel_multiplier=-1).then_inc(p1_sel, 1)

            pool_rstd("att1", n, 0)
            yield
            pool_rstd("att1", n, 1)
            for _ in range(11):
                yield
            for p in range(NP + 2):
                if p >= 2:
                    select(p - 2)
                yield
                if p < NP:
                    w = KEY_PIECES[p][2] - KEY_PIECES[p][1]
                    pool.wait_ge(sq_ready, NP * n + p + 1)
                    pool.tensor_tensor(sq[:, p % 2, 0, 0:w], sq[:, p % 2, 0, 0:w],
                                       sq[:, p % 2, 1, 0:w], ALU.add).then_inc(sum_ready, 1)
                yield
                yield

        def pool_ffn(s, src, n, half=None):
            pool = nc.gpsimd

            def difference(h):
                if h == 1:
                    pool.wait_ge(xr_ready[s], 2 * n + 1)
                    if half is not None:
                        pool.wait_ge(x_added[s], 2 * n + 1)
                for c in range(NC):
                    pool.wait_ge(xt_ready[s], 4 * n + 2 * h + c + 1)
                    pool.tensor_tensor(diff[:, c, :], xtb[:, c, 1 + HALF * h:1 + HALF * (h + 1)],
                                       xtb[:, c, HALF * h:HALF * (h + 1)],
                                       ALU.subtract).then_inc(diff_done[s], 1)

            def square_k(h, j):
                pool.wait_ge(kr_ready[s], 4 * n + 2 * h + j + 1)
                pool.tensor_tensor(ka[:, j, :], kr[:, j, :], kr[:, j, :],
                                   ALU.mult).then_inc(ka_ready[s], 1)

            def add(h):
                for j in range(2):
                    pool.wait_ge(tm_ready[s], 4 * n + 2 * h + j + 1)
                    pair = src[:, TPH * h + 2 * j:TPH * h + 2 * j + 2, :]
                    last = pool.tensor_tensor(pair, pair, tm[:, 2 * j:2 * j + 2, :], ALU.add)
                last.then_inc(x_added[s], 1)

            if half is not None:
                pool_rstd(s, n, half)
                yield
                yield
                difference(half)
                yield
                yield
                yield
                square_k(half, 0)
                yield
                square_k(half, 1)
                yield
                yield
                yield
                yield
                add(half)
                yield
                return
            pool_rstd(s, n, 0)
            yield
            pool_rstd(s, n, 1)
            yield
            yield
            difference(0)
            yield
            yield
            yield
            square_k(0, 0)
            yield
            square_k(0, 1)
            yield
            difference(1)
            yield
            yield
            yield
            add(0)
            yield
            square_k(1, 0)
            yield
            square_k(1, 1)
            yield
            yield
            yield
            add(1)
            yield

        def pool_proj3(n):
            pool_rstd("proj3", n, 0)
            yield
            pool_rstd("proj3", n, 1)
            yield
            yield
            yield
            yield
            yield
            for j in range(8):
                nc.gpsimd.wait_ge(mid_done, 8 * n + j + 1)
                nc.gpsimd.tensor_tensor(parts[:, j % 2, LO, :], x32[:, j % 2, :], parts[:, j % 2, MID, :],
                                        ALU.subtract).then_inc(lo_done, 1)
                yield
            yield

        def sp_att1(n):
            if isinstance(n, int) and n < 2:
                for h in range(2):
                    sp_load(n, h)
            for _ in range(N_ATT1):
                yield

        def sp_proj3(n):
            for _ in range(6):
                yield
            for j in range(8):
                h, kq, ht = j // 4, (j // NHT) % 2, j % NHT
                nc.sync.wait_ge(lo_done, 8 * n + j + 1)
                nc.sync.dma_start(
                    parts_dram[n, kq, ht].rearrange("r d h n -> (d h) r n")[:, :, HALF * h:HALF * (h + 1)],
                    parts[:, j % 2, :, :]).then_inc(part_stored[j % 2], 16)
                yield
            for g in ((0, 1, 2) if isinstance(n, int) and n == 0 else (1, 2)):
                sp_stack(n, g)
            yield

        def sp_load(n, h):
            if not (isinstance(n, int) and n == 0):
                nc.sync.wait_ge(xb_copied[h], 16 * n)
                nc.sync.wait_ge(xh_ready["proj3"], 2 * n)
            nc.sync.dma_start(xa[:, TPH * h:TPH * (h + 1), :],
                              x_tok[n][:, TPH * h:TPH * (h + 1), :]).then_inc(x_loaded[h], 16)

        def sp_copy(n, h):
            nc.sync.wait_ge(x_added["ffn2"], 2 * n + h + 1)
            if not (isinstance(n, int) and n == 0):
                nc.sync.wait_ge(out_stored[h], 16 * n)
            nc.sync.dma_start(xb[:, TPH * h:TPH * (h + 1), :], xa[:, TPH * h:TPH * (h + 1), :]
                              ).then_inc(xb_copied[h], 16)

        def sp_store(n, h):
            nc.sync.wait_ge(x_added["ffn4"], 2 * n + h + 1)
            nc.sync.dma_start(out_tok[n][:, TPH * h:TPH * (h + 1), :], xb[:, TPH * h:TPH * (h + 1), :]
                              ).then_inc(out_stored[h], 16)

        def sp_stack(n, g):
            r = STACK_OF[g]
            ht, h0 = g // 2, GH * (g % 2)
            if g == 3:
                nc.sync.wait_ge(s_full, GH * NP * (NG * n + 1))
            elif not (isinstance(n, int) and n == 0):
                nc.sync.wait_ge(s_full, GH * NP * (NG * (n - 1) + (NG if g == 0 else g + 1)))
            for k in range(2):
                nc.sync.wait_ge(part_stored[k], 64 * n + 64)
            src = parts_dram[n]

            def copy(to, kq, slot, part, count):
                nc.sync.dma_start(
                    to[HD * slot:HD * (slot + count), :, :],
                    src[kq, ht, part:part + count].rearrange("r d h n -> (r d) h n")[:, h0:h0 + GH, :]
                ).then_inc(stack_ready[r], 16)

            copy(ks[r], 0, 0, HI, 3)
            copy(ks[r], 0, 3, HI, 2)
            copy(ks[r], 0, 5, HI, 1)
            for slot, part in enumerate(Q_SLOTS):
                copy(qs[r], 1, slot, part, 1)

        emptied = [None, None]

        def side_job(k, taken, value):
            if emptied[k] is not None:
                nc.tensor.wait_ge(*emptied[k])
            emptied[k] = (taken, value)
            return side[k]

        def pe_transposed(s, src, n, h):
            nc.tensor.wait_ge(xh_ready[s], 2 * n + h + 1)
            for c in range(NC):
                bank = side_job(c, xt_ready[s], 4 * n + 2 * h + c + 1)
                for t in range(TPH):
                    mm = nc.tensor.transpose(bank[:, P * t:P * (t + 1)], src[:, t, P * c:P * (c + 1)],
                                             ident[:, :])
                mm.then_inc(tr_full[s], 1)

        def pe_att1(n):
            pe = nc.tensor

            def values(t):
                if t % TPH == 0:
                    pe.wait_ge(xt_ready["att1"], 4 * n + 2 * (t // TPH) + 2)
                bank = side_job(t % 2, vp_ready, 8 * n + t + 1)
                for c in range(NC):
                    mm = pe.matmul(bank[:, 0:C + 3], xta[:, c, P * t:P * (t + 1)], wvp[:, c, :],
                                   start=(c == 0), stop=(c == NC - 1))
                mm.then_inc(v1_full, 1)

            def positions(c, h):
                pe.wait_ge(vp_ready, 8 * n + TPH * (h + 1))
                bank = side_job((3 * h + c) % 2, pb_ready, 6 * n + 3 * h + c + 1)
                for t in range(TPH):
                    mm = pe.transpose(bank[:, P * t:P * (t + 1)],
                                      vp[:, TPH * h + t, POS + c:POS + c + 1].to_broadcast([P, P]),
                                      ident[:, :])
                mm.then_inc(pb_full, 1)

            def attend(t):
                m = t + 1 if t < TPH else TPH + t + 1
                pe.wait_ge(p1_exp, NP * n + m)
                pe.wait_ge(p1_sel, NT * n + t + 1)
                bank = side_job(t % 2, x1_done, 8 * n + t + 1)
                for kt in range(t + 1):
                    at = P1_AT[kt] + P * (t - kt)
                    mm = pe.matmul(bank[:, 0:VC], p1[:, at:at + P], vp[:, kt, :],
                                   start=(kt == 0), stop=(kt == t))
                mm.then_inc(pv1_full, 1)

            yield
            yield
            pe_transposed("att1", xha, n, 0)
            yield
            yield
            pe_transposed("att1", xha, n, 1)
            yield
            for t in range(0, NT, 2):
                values(t)
                values(t + 1)
                yield
            for c, h in ((0, 0), (2, 0), (1, 1)):
                positions(c, h)
                positions((c + 1) % 3, h if c < 2 else 1)
                yield
            for p in range(NP + 2):
                yield
                for t in summed_after(p):
                    attend(t)
                yield
                yield

        def pe_ffn(s, n, half=None):
            pe = nc.tensor

            def keys(h, j):
                pe.wait_ge(xk_ready[s], 2 * n + h + 1)
                bank = side_job(j, kr_ready[s], 4 * n + 2 * h + j + 1)
                for c in range(NC):
                    mm = pe.matmul(bank[:, :], wkT[:, c, P * j:P * (j + 1)], xk[:, c, :],
                                   start=(c == 0), stop=(c == NC - 1))
                mm.then_inc(k_full[s], 1)

            def pair(h, j, lhs, rhs, full, taken):
                bank = side_job(j, taken, 4 * n + 2 * h + j + 1)
                for t in range(2):
                    at = P * (2 * j + t)
                    for c in range(NC):
                        mm = pe.matmul(bank[:, C * t:C * (t + 1)], lhs[:, c, at:at + P], rhs[:, c, :],
                                       start=(c == 0), stop=(c == NC - 1))
                mm.then_inc(full, 1)

            def receptance(h, j):
                pe.wait_ge(xr_ready[s], 2 * n + h + 1)
                pair(h, j, xr, wrT, r_full[s], rexp_done[s])

            def values(h, j):
                pe.wait_ge(ka_ready[s], 4 * n + 2 * h + 2)
                pair(h, j, ka, wvT, v_full[s], tm_ready[s])

            yield
            yield
            pe_transposed(s, xhb, n, half or 0)
            yield
            yield
            if half is None:
                pe_transposed(s, xhb, n, 1)
                yield
            for h in (range(2) if half is None else (half,)):
                for product in (keys, receptance, values):
                    for j in range(2):
                        product(h, j)
                        yield
            if half is not None:
                yield

        def pe_proj3(n):
            pe = nc.tensor
            yield
            yield
            pe_transposed("proj3", xha, n, 0)
            yield
            yield
            pe_transposed("proj3", xha, n, 1)
            yield
            for j in range(8):
                h, kq, ht = j // 4, (j // NHT) % 2, j % NHT
                pe.wait_ge(xt_ready["proj3"], 4 * n + 2 * h + 2)
                bank = side_job(j % 2, x32_ready, 8 * n + j + 1)
                for c in range(NC):
                    mm = pe.matmul(bank[:, :], wkq[:, c, kq, ht, :, :], xta[:, c, HALF * h:HALF * (h + 1)],
                                   start=(c == 0), stop=(c == NC - 1))
                mm.then_inc(kq_full, 1)
                yield
            yield
            yield

        def pe_values3(n):
            for j in range(4):
                bank = side_job(j % 2, v3_ready, 4 * n + j + 1)
                for t in range(2):
                    at = P * (2 * j + t)
                    for c in range(NC):
                        mm = nc.tensor.matmul(bank[:, C * t:C * (t + 1)], xta[:, c, at:at + P],
                                              wv3[:, c, :, :], start=(c == 0), stop=(c == NC - 1))
                mm.then_inc(v3_full, 1)
            yield

        def negmax_group(t, s):
            g, late = divmod(t - NP, NP)
            return g if s == 1 and late == 0 and 0 <= g < NG else None

        def output_group(t, s, h):
            g, late = divmod(t - LEAD - (NP + 2 if h else TPH + 2), NP)
            return g if s == 0 and late == 0 and 0 <= g < NG else None

        def pe_att3(i, t, s):
            pe = nc.tensor
            heads = range(2 * s, 2 * s + 2)
            e = t - LEAD
            if t < NG * NP and s == 0 and t % NP == 0:
                g = t // NP
                r = STACK_OF[g]
                pe.wait_ge(stack_ready[r], 16 * N_STACK_DMA * (STACK_LOADS[r] * i + STACK_NTH[g] + 1))
            if 0 <= e < NG * NP and s == 0 and e % NP == 0:
                pe.wait_ge(crow_ready, 32 * (NG * i + e // NP + 1))
            for j in heads:
                if t < NG * NP:
                    g, m = divmod(t, NP)
                    tile, k0, k1 = QUERY_PIECES[m]
                    r = STACK_OF[g]
                    k = GH * t + j
                    pe.wait_ge(max_free, GH * NG * NP * i + max(0, k + 1 - MAX_BANKS))
                    pe.matmul(max_bank[k % MAX_BANKS][:, 0:k1 - k0], qs[r][0:KROWS, j, P * tile:P * (tile + 1)],
                              ks[r][0:KROWS, j, k0:k1], start=True, stop=True).then_inc(max_full, 1)
                if 0 <= e < NG * NP:
                    g, m = divmod(e, NP)
                    kt, q0, q1 = KEY_PIECES[m]
                    r = STACK_OF[g]
                    k = GH * e + j
                    pe.wait_ge(exp_done, GH * NG * NP * i + max(0, k + 1 - EXP_BANKS))
                    pe.matmul(exp_bank[k % EXP_BANKS][:, 0:q1 - q0], ks[r][:, j, P * kt:P * (kt + 1)],
                              qs[r][:, j, q0:q1], start=True, stop=True).then_inc(s_full, 1)
            if s == 1 and 1 <= e <= NG * NP:
                g, m = divmod(e - 1, NP)
                kt, q0, q1 = KEY_PIECES[m]
                h = 0 if m < TPH else 1
                pe.wait_ge(exp_done, GH * (NG * NP * i + e))
                if DIAGONAL[m]:
                    pe.wait_ge(sel_done, NG * NT * i + NT * g + NTH_DIAGONAL[m] + 1)
                if kt == 0:
                    pe.wait_ge(ot_ready, 8 * i + 2 * g + h)
                for j in range(GH):
                    mm = pe.matmul(o_bank[32 * j:32 * j + VW, q0 - HALF * h:q1 - HALF * h],
                                   v3[:, kt, GH * g + j, :], pt[:, (e - 1) % 2, j, 0:q1 - q0],
                                   start=(kt == 0), stop=(q1 - q0 == P), skip_group_check=True)
                mm.then_inc(pv_done, 1)

        def pe_rows3(i, t, s):
            pe = nc.tensor
            g = negmax_group(t, s)
            if g is not None:
                pe.wait_ge(negmax_ready, NG * i + g + 1)
                bank = side_job(g % 2, negmaxT_ready, NG * i + g + 1)[:, :].bitcast(BF16)
                for c in range(2):
                    mm = pe.transpose(bank[0:GH * NT, P * c:P * (c + 1)],
                                      neg_max[:, c, :, :].rearrange("p j t -> p (j t)"), identb[:, :])
                mm.then_inc(negmaxT_full, 1)
            for h in range(2):
                g = output_group(t, s, h)
                if g is not None:
                    pe.wait_ge(ot_ready, 8 * i + 2 * g + h + 1)
                    bank = side_job(h, on_ready, 8 * i + 2 * g + h + 1)
                    for q in range(TPH):
                        mm = pe.transpose(bank[:, P * q:P * (q + 1)], ot[:, h, P * q:P * (q + 1)], ident[:, :])
                    mm.then_inc(on_full, 1)

        def act_att3(i, t, s):
            act = nc.scalar
            e = t - LEAD
            if 0 <= e < NG * NP:
                m = e % NP
                kt, q0, q1 = KEY_PIECES[m]
                if s == 0:
                    act.wait_ge(pv_done, NG * NP * i + max(0, e - 1))
                for j in range(2 * s, 2 * s + 2):
                    k = GH * e + j
                    act.wait_ge(s_full, GH * NG * NP * i + k + 1)
                    act.activation(pt[:, e % 2, j, 0:q1 - q0], exp_bank[k % EXP_BANKS][:, 0:q1 - q0], ACT.Exp,
                                   scale=SCALE).then_inc(exp_done, 1)
            if s == 1:
                return
            for h, at in ((0, TPH + 1), (1, NP + 1)):
                if e >= at and (e - at) % NP == 0 and (e - at) // NP < NG:
                    g = (e - at) // NP
                    act.wait_ge(pv_done, NG * NP * i + NP * g + (TPH if h == 0 else NP))
                    act.wait_ge(on_full, 8 * i + max(0, 2 * g + h - 1))
                    act.activation(ot[:, h, :], o_bank[:, :], ACT.Copy).then_inc(ot_ready, 1)

        def dve_att3(i, t, s):
            dve = nc.vector
            if t < NG * NP:
                g, m = divmod(t, NP)
                tile, k0, k1 = QUERY_PIECES[m]
                w = k1 - k0
                if m == 0 and s == 0:
                    dve.wait_ge(negmax_ready, NG * i + g)
                for j in range(2 * s, 2 * s + 2):
                    k = GH * t + j
                    dve.wait_ge(max_full, GH * NG * NP * i + k + 1).then_inc(scores_seen, 1)
                    if k1 == P * (tile + 1):
                        dve.tensor_tensor_reduce(max_bank[k % MAX_BANKS][:, 0:w], max_bank[k % MAX_BANKS][:, 0:w],
                                                 mask[:, HALF - w:HALF], 1.0, LOWEST, ALU.add, ALU.max,
                                                 piece_max[:, j, m:m + 1]).then_inc(max_free, 1)
                    else:
                        dve.tensor_reduce(piece_max[:, j, m:m + 1], max_bank[k % MAX_BANKS][:, 0:w], AX.X,
                                          ALU.max).then_inc(max_free, 1)
                if m == NP - 1 and s == 1:
                    base = 2 * (NG * i + g)
                    dve.wait_ge(max_free, GH * (NG * NP * i + t + 1))
                    dve.tensor_tensor(piece_max[:, :, TPH:NT], piece_max[:, :, TPH:NT],
                                      piece_max[:, :, NT:NP], ALU.max).then_inc(c_step, 1)
                    dve.wait_ge(c_step, base + 1)
                    dve.tensor_scalar(neg_max[:, 0, :, :], piece_max[:, :, 0:NT], -1.0, None,
                                      ALU.mult).then_inc(c_step, 1)
                    dve.wait_ge(c_step, base + 2)
                    dve.scalar_tensor_tensor(out=neg_max[:, 1, :, :], in0=piece_max[:, :, 0:NT],
                                             scalar=-1.0, in1=neg_max[:, 0, :, :], op0=ALU.mult,
                                             op1=ALU.subtract).then_inc(negmax_ready, 1)

        def dve_rows3(i, t, s):
            dve = nc.vector
            g = negmax_group(t, s)
            if g is not None:
                dve.wait_ge(negmaxT_full, NG * i + g + 1)
                dve.wait_ge(crow_ready, 32 * (NG * i + g))
                bank = side[g % 2][:, :].bitcast(BF16)
                dve.tensor_copy(neg_maxT[:, :, :],
                                bank[0:GH * NT, 0:2 * P].rearrange("p (c n) -> p c n", c=2)
                                ).then_inc(negmaxT_ready, 1)
            for h in range(2):
                g = output_group(t, s, h)
                if g is not None:
                    n = 8 * i + 2 * g + h
                    dve.wait_ge(on_full, n + 1)
                    o = side[h][:, :].rearrange("p (t j d) -> p t j d", t=TPH, j=GH)
                    dve.wait_ge(on_ready, n)
                    dve.reciprocal(rsum[:, :, :], o[:, :, :, HD]).then_inc(rsum_done, 1)
                    dve.wait_ge(rsum_done, n + 1)
                    dve.wait_ge(xb_added, n)
                    dve.tensor_tensor(on[:, :, :, :], o[:, :, :, 0:HD],
                                      rsum[:, :, :].unsqueeze(3).to_broadcast([P, TPH, GH, HD]),
                                      ALU.mult).then_inc(on_ready, 1)

        def pool_att3(i, t, s):
            pool = nc.gpsimd
            e = t - LEAD
            if s == 1 and 0 <= e < NG * NP and DIAGONAL[e % NP]:
                block = pt[:, e % 2, :, 0:P]
                pool.wait_ge(exp_done, GH * (NG * NP * i + e + 1)).then_inc(exp_seen, 1)
                pool.affine_select(out=block, in_=block, compare_op=ALU.is_ge, fill=0.0, base=0,
                                   pattern=[[0, GH], [1, P]], channel_multiplier=-1).then_inc(sel_done, 1)

        def pool_rows3(i, t, s):
            pool = nc.gpsimd
            for h in range(2):
                g = output_group(t, s, h)
                if g is not None:
                    pool.wait_ge(on_ready, 8 * i + 2 * g + h + 1)
                    pool.wait_ge(xb_copied[h], 16 * i + 16)
                    x_half = xb[:, TPH * h:TPH * (h + 1), GH * HD * g:GH * HD * (g + 1)]
                    pool.tensor_tensor(x_half, x_half, on[:, :, :, :].rearrange("p t j d -> p t (j d)"),
                                       ALU.add).then_inc(xb_added, 1)

        def sp_rows3(i, t, s):
            g = negmax_group(t, s)
            if g is not None:
                r = STACK_OF[g]
                nc.sync.wait_ge(negmaxT_ready, NG * i + g + 1)
                for c in range(2):
                    nc.sync.dma_start(qs[r][KROWS + c:KROWS + c + 1, :, :], neg_maxT[:, c, :]
                                      ).then_inc(crow_ready, 16)
            if t == LEAD + NP and s == 0:
                sp_stack(i, 3)

        def chain(*stages):
            for stage in stages:
                yield from stage

        def run(chunks):
            for _ in chunks:
                pass

        def has_rows(u):
            t, s = divmod(u, 2)
            return negmax_group(t, s) is not None or any(output_group(t, s, h) is not None for h in range(2))

        def places(front, back):
            free = [u for u in range(2 * SLOTS) if not has_rows(u)]
            dense = [u for u in free if u < DENSE][:front]
            rest, sparse = [u for u in free if u < BACK][len(dense):], front - len(dense)
            return dense + [rest[len(rest) * k // sparse] for k in range(sparse)] + \
                [u for u in free if u >= BACK][:back]

        def attend_with(att, rows, i, chunks, front, back):
            at = places(front, back)
            assert len(at) == len(set(at)) == front + back and max(at) < 2 * SLOTS
            for u in range(2 * SLOTS):
                t, s = divmod(u, 2)
                att(i, t, s)
                rows(i, t, s)
                if u in at:
                    next(chunks)

        N_ATT1, N_FFN, N_HALF_FFN, N_PROJ3 = 12 + 3 * (NP + 2), 17, 11, 15
        N_BEFORE = N_ATT1 + N_FFN + N_PROJ3
        N_LAST = 4

        def schedule(eng, att, rows, before, first, ffn4, last, enter=None):
            def attend(i, chunks, front):
                attend_with(att, rows, i, chunks, front, N_HALF_FFN)

            run(before(0))
            run(first(0))
            attend(0, chain(before(1), ffn4(0, 0)), N_BEFORE)
            run(first(1))
            with eng.Fori(0, B - 2) as r:
                if enter:
                    enter(r + 1)
                attend(r + 1, chain(ffn4(r, 1), last(r), before(r + 2), ffn4(r + 1, 0)),
                       N_HALF_FFN + N_LAST + N_BEFORE)
                run(first(r + 2))
            if enter:
                enter(B - 1)
            attend(B - 1, chain(ffn4(B - 2, 1), last(B - 2), ffn4(B - 1, 0)), N_HALF_FFN + N_LAST)
            run(ffn4(B - 1, 1))
            run(last(B - 1))

        def nothing(n):
            yield

        def idle(n):
            for _ in range(N_LAST):
                yield

        def no_ffn(n, half=None):
            for _ in range(N_FFN if half is None else N_HALF_FFN):
                yield

        block = ctx.enter_context(nc.Block())

        @block.sync
        def _(sp):
            for k, w in enumerate((wv, wo, w_r, w_k, w_v)):
                sp.dma_start(raw[:, k, :, :], w.rearrange("(a p) c -> p a c", p=P)).then_inc(raw_loaded, 16)
            sp.dma_start(raw3d, w3d).then_inc(raw_loaded, 16)
            for a in range(NC):
                sp.dma_start(raw_kqv[:, a, :, :],
                             wkqv[:, P * a:P * (a + 1), :].rearrange("h c f -> c h f")).then_inc(raw_loaded, 16)
            for row, v in ((bv_row, bv), (mur_row, mu_r), (muk_row, mu_k)):
                sp.dma_start(row, v.rearrange("(a n) -> a n", a=1)).then_inc(rows_loaded, 16)
            sp.dma_start(rows[:, 3 * C:3 * C + H * 48],
                         bkqv.rearrange("(a h) f -> a (h f)", a=1)).then_inc(rows_loaded, 16)
            sp.dma_start(bo_all, bo.rearrange("(a n) -> a n", a=1).to_broadcast([P, C])).then_inc(rows_loaded, 16)
            sp.dma_start(bias_vp[:, C:C + 3],
                         b3d.rearrange("(a n) -> a n", a=1).to_broadcast([P, 3])).then_inc(rows_loaded, 16)
            sp.dma_start(bv3[:, :, :], bkqv[:, 2 * HD:3 * HD].unsqueeze(0).to_broadcast([P, H, HD])
                         ).then_inc(rows_loaded, 16)

            def before(n):
                return chain(sp_att1(n), no_ffn(n), sp_proj3(n))

            def first(n):
                if isinstance(n, int) and n == 0:
                    for h in range(2):
                        sp_copy(0, h)
                else:
                    sp_stack(n, 0)
                yield

            def last(n):
                for h in range(2):
                    sp_store(n, h)
                    if not (isinstance(n, int) and n == B - 1):
                        sp_copy(n + 1, h)
                    if not isinstance(n, int):
                        sp_load(n + 2, h)
                for _ in range(N_LAST):
                    yield

            schedule(sp, lambda i, t, s: None, sp_rows3, before, first, no_ffn, last)
            for h in range(2):
                sp.wait_ge(out_stored[h], 16 * B)

        @block.gpsimd
        def _(pool):
            for m in (ident, identb, mask):
                pool.memset(m[:, :], 0.0).then_inc(cleared, 1)
            pool.wait_ge(cleared, 3)
            for m in (ident, identb):
                pool.affine_select(out=m[:, :], in_=m[:, :], compare_op=ALU.not_equal, fill=1.0, base=0,
                                   pattern=[[-1, P]], channel_multiplier=1).then_inc(consts_ready, 1)
            tail = mask[:, HALF - P:HALF]
            pool.affine_select(out=tail, in_=tail, compare_op=ALU.is_ge, fill=LOWEST, base=0,
                               pattern=[[-1, P]], channel_multiplier=1).then_inc(consts_ready, 1)
            pool.memset(minus_half[:, :], -0.5).then_inc(consts_ready, 1)
            pool.memset(xtb[:, :, 0:1], 0.0).then_inc(consts_ready, 1)
            pool.memset(vp[:, :, ONE:ONE + 1], 1.0).then_inc(consts_ready, 1)
            pool.memset(v3[:, :, :, HD:VW], 1.0).then_inc(consts_ready, 1)
            pool.wait_ge(consts_ready, 7)
            for r in range(STACKS):
                pool.memset(ks[r][KROWS:SROWS, :, :], 1.0).then_inc(rows_of_ones, 1)

            def before(n):
                return chain(pool_att1(n), pool_ffn("ffn2", xa, n), pool_proj3(n))

            pool.wait_ge(rows_of_ones, STACKS)
            pool.wait_ge(weights_ready, 1)
            schedule(pool, pool_att3, pool_rows3, before, nothing, lambda n, h: pool_ffn("ffn4", xb, n, h), idle)

        @block.scalar
        def _(act):
            def before(n):
                return chain(act_att1(n), act_ffn("ffn2", n), act_proj3(n))

            act.preload_act_table_set("natural_log_exp_and_others")
            act.wait_ge(weights_ready, 1)
            schedule(act, act_att3, lambda i, t, s: None, before, nothing,
                     lambda n, h: act_ffn("ffn4", n, h), idle)

        @block.vector
        def _(dve):
            dve.memset(o_bank[:, :], 0.0)
            dve.wait_ge(raw_loaded, 16 * 8)
            dve.wait_ge(rows_loaded, 16 * 7)
            for q in range(2):
                dve.tensor_copy(bkq_row[:, q, :, :, :],
                                kqv_row[:, :, :, HD * q:HD * (q + 1)].rearrange("p t h d -> p t d h")
                                ).then_inc(rows_ready, 1)
            kqv = raw_kqv.rearrange("p a (t h) f -> p a t h f", t=NHT)
            for a in range(NC):
                for q in range(2):
                    for t in range(NHT):
                        dve.tensor_copy(wkq[:, a, q, t, :, :],
                                        kqv[:, a, t, :, HD * q:HD * (q + 1)].rearrange("p h d -> p d h"))
            dve.tensor_copy(wv3[:, :, :, :], raw_kqv[:, :, :, 2 * HD:3 * HD])
            job = 0
            for dst in (wvp, wrT, wkT, wvT):
                for a in range(NC):
                    dve.wait_ge(setup_full, job + 1)
                    dve.tensor_copy(dst[:, a, 0:C], side[job % 2][:, 0:C]).then_inc(setup_taken, 1)
                    job += 1
            dve.wait_ge(setup_full, job + 1)
            dve.tensor_copy(cols[:, :], side[job % 2][:, 0:10]).then_inc(setup_taken, 1)
            job += 1
            dve.memset(bv_wide, 1.0).then_inc(bv_spread, 1)
            dve.wait_ge(setup_taken, job)
            dve.wait_ge(bv_spread, 1)
            for a in range(NC):
                dve.tensor_scalar(bv_wide[:, a, :], bv_wide[:, a, :], cols[:, BV + a:BV + a + 1], None,
                                  ALU.mult).then_inc(bv_spread, 1)
            dve.wait_ge(setup_full, job + 1)
            dve.tensor_copy(wvp[:, :, C:C + 3],
                            side[job % 2][:, 0:3 * NC].rearrange("p (a k) -> p a k", a=NC)
                            ).then_inc(setup_taken, 1)
            job += 1
            dve.wait_ge(setup_full, job + 1)
            dve.tensor_tensor(bias_vp[:, 0:C], side[job % 2][:, 0:C], bo_all, ALU.add).then_inc(setup_taken, 1)
            job += 1
            dve.wait_ge(setup_full, job + 2)
            for a in range(NC):
                dve.tensor_copy(wvp[:, a, 0:C], side[job % 2][:, 0:C]).then_inc(setup_taken, 1)
                job += 1
            dve.memset(rinv1[:, :], 0.0).then_inc(weights_ready, 1)
            dve.wait_ge(weights_ready, 1)
            dve.wait_ge(consts_ready, 7)

            def before(n):
                return chain(dve_att1(n), dve_ffn("ffn2", xa, n), dve_proj3(n))

            schedule(dve, dve_att3, dve_rows3, before, dve_values3,
                     lambda n, h: dve_ffn("ffn4", xb, n, h), idle)

        @block.tensor
        def _(pe):
            pe.wait_ge(consts_ready, 2)
            pe.wait_ge(raw_loaded, 16 * 8)
            pe.wait_ge(rows_loaded, 16 * 7)
            pe.wait_ge(rows_ready, 2)
            jobs = [0]

            def setup_job():
                jobs[0] += 1
                return side_job((jobs[0] - 1) % 2, setup_taken, jobs[0])

            for k in (1, 2, 3, 4):
                for c in range(NC):
                    bank = setup_job()
                    for a in range(NC):
                        mm = pe.transpose(bank[:, P * a:P * (a + 1)], raw[:, k, a, P * c:P * (c + 1)], ident[:, :])
                    mm.then_inc(setup_full, 1)
            bank = setup_job()
            pieces = [row[:, P * a:P * (a + 1)] for row in (bv_row, mur_row, muk_row) for a in range(NC)]
            pieces += [bkq_row[:, q, t, :, :] for q in range(2) for t in range(NHT)]
            for k, piece in enumerate(pieces):
                mm = pe.matmul(bank[:, k:k + 1], piece, ident[0:1, 0:1], start=True, stop=True)
            mm.then_inc(setup_full, 1)
            bank = setup_job()
            for a in range(NC):
                mm = pe.transpose(bank[:, 3 * a:3 * (a + 1)], raw3d[:, P * a:P * (a + 1)], ident[0:3, 0:3])
            mm.then_inc(setup_full, 1)
            pe.wait_ge(bv_spread, 3)
            bank = setup_job()
            for a in range(NC):
                mm = pe.matmul(bank[:, 0:C], bv_wide[:, a, :], wvp[:, a, 0:C], start=(a == 0), stop=(a == NC - 1))
            mm.then_inc(setup_full, 1)
            for c in range(NC):
                bank = setup_job()
                for a in range(NC):
                    mm = pe.matmul(bank[:, 0:C], raw[:, 0, a, P * c:P * (c + 1)], wvp[:, a, 0:C],
                                   start=(a == 0), stop=(a == NC - 1))
                mm.then_inc(setup_full, 1)
            pe.wait_ge(weights_ready, 1)
            pe.wait_ge(consts_ready, 7)
            pe.wait_ge(rows_of_ones, STACKS)

            def enter(n):
                for k in range(2):
                    emptied[k] = (v3_ready, 4 * n + 3 + k)

            def before(n):
                return chain(pe_att1(n), pe_ffn("ffn2", n), pe_proj3(n))

            schedule(pe, pe_att3, pe_rows3, before, pe_values3, lambda n, h: pe_ffn("ffn4", n, h), idle, enter)


_INS = ['L0_attn_a_x', 'L0_attn_a_wq', 'L0_attn_a_bq', 'L0_attn_a_wk', 'L0_attn_a_bk', 'L0_attn_a_wv',
        'L0_attn_a_bv', 'L0_attn_a_wo', 'L0_attn_a_bo', 'L0_attn_a_w3d', 'L0_attn_a_b3d',
        'L0_attn_b_Wkqv', 'L0_attn_b_bkqv', 'L0_ffn_W_r', 'L0_ffn_W_k', 'L0_ffn_W_v', 'L0_ffn_mu_r',
        'L0_ffn_mu_k']
_OUTS = [((B, S, C), 'float32')]


def kernel(**inputs):
    import numpy as _np
    import concourse.bacc as _bacc
    from concourse import mybir as _mybir
    from concourse.bass_utils import run_bass_kernel_spmd as _run

    nc = _bacc.Bacc("TRN2", target_bir_lowering=False, num_devices=1)
    arrays, args = {}, []
    for name in _INS:
        a = _np.ascontiguousarray(inputs[name])
        arrays[f"in_{name}_dram"] = a
        args.append(nc.dram_tensor(f"in_{name}_dram", a.shape, _mybir.dt.from_np(a.dtype), kind="ExternalInput").ap())
    for i, (shape, dtype) in enumerate(_OUTS):
        dt = _mybir.dt.from_np(_np.dtype(dtype))
        args.append(nc.dram_tensor(f"out_{i}_dram", shape, dt, kind="ExternalOutput").ap())
    bass_hybrid(nc, *args)
    r = _run(nc, [arrays], core_ids=[0])
    return r.results[0]["out_0_dram"]
```
